# Optimizing a Trainium2 kernel written in Bass

```python
import numpy as np
import jax
import jax.numpy as jnp

def _softmax(x, axis=-1):
    return jax.nn.softmax(x, axis=axis)

def _gelu(x):
    return jax.nn.gelu(x, approximate=True)

def _silu(x):
    return jax.nn.silu(x)

def _sigmoid(x):
    return jax.nn.sigmoid(x)

def _layernorm(x, axis=-1, eps=1e-05):
    m = jnp.mean(x, axis=axis, keepdims=True)
    v = jnp.var(x, axis=axis, keepdims=True)
    return (x - m) / jnp.sqrt(v + eps)

def _scatter_add(tgt, idx, src, axis=0):
    return tgt.at[idx].add(src)

def _segment_sum(src, seg, n):
    return jax.ops.segment_sum(src, seg, n)
kernel_name = 'mk_seq_preln_d4_jaxref_r8_472acb'

def setup_inputs(seed: int=0):
    np.random.seed(seed)
    _w = jnp.asarray

    def _L0_attn_setup():
        import jax, jax.numpy as jnp
        import numpy as np
        D_MODEL = 128
        N_HEADS = 16
        D_HEAD = 64
        B, S = (8, 128)
        EPS = 1.1920929e-07
        key = jax.random.key(seed)
        k1, k2, k3 = jax.random.split(key, 3)
        x = jax.random.normal(k1, (B, S, D_MODEL), dtype=jnp.float32)
        W_qkv = jax.random.normal(k2, (3 * N_HEADS * D_HEAD, D_MODEL), dtype=jnp.float32) * 0.02
        b_qkv = jnp.zeros((3 * N_HEADS * D_HEAD,), dtype=jnp.float32)
        W_o = jax.random.normal(k3, (D_MODEL, N_HEADS * D_HEAD), dtype=jnp.float32) * 0.02
        b_o = jnp.zeros((D_MODEL,), dtype=jnp.float32)
        return {'x': x, 'W_qkv': W_qkv, 'b_qkv': b_qkv, 'W_o': W_o, 'b_o': b_o}
    _L0_attn_in = _L0_attn_setup()

    def _L0_ffn_setup():
        import jax, jax.numpy as jnp
        import numpy as np
        DIM = 128
        HIDDEN = 384
        SCALE = 1.0 / 127.0

        def _dequant(w_int, dtype):
            return w_int.astype(dtype) * jnp.asarray(SCALE, dtype)
        key = jax.random.key(seed)
        k_x, k_g, k_u, k_d = jax.random.split(key, 4)
        x = jax.random.normal(k_x, (4, 256, DIM), dtype=jnp.float32)
        w_gate = jax.random.randint(k_g, (HIDDEN, DIM), -127, 128, dtype=jnp.int32)
        w_up = jax.random.randint(k_u, (HIDDEN, DIM), -127, 128, dtype=jnp.int32)
        w_down = jax.random.randint(k_d, (DIM, HIDDEN), -127, 128, dtype=jnp.int32)
        return {'x': x, 'w_gate': w_gate, 'w_up': w_up, 'w_down': w_down}
    _L0_ffn_in = _L0_ffn_setup()

    def _L1_attn_setup():
        import jax, jax.numpy as jnp
        import numpy as np
        from math import sqrt
        EMBED = 128
        HEADS = 16
        key = jax.random.key(seed)
        k1, k2, k3, k4, k5 = jax.random.split(key, 5)
        x = jax.random.normal(k1, (2, 256, EMBED), dtype=jnp.float32)
        s = 1.0 / sqrt(EMBED)
        W_qkv = jax.random.normal(k2, (EMBED, 3 * EMBED), dtype=jnp.float32) * s
        b_qkv = jax.random.normal(k3, (3 * EMBED,), dtype=jnp.float32) * 0.01
        W_out = jax.random.normal(k4, (EMBED, EMBED), dtype=jnp.float32) * s
        b_out = jax.random.normal(k5, (EMBED,), dtype=jnp.float32) * 0.01
        return {'x': x, 'W_qkv': W_qkv, 'b_qkv': b_qkv, 'W_out': W_out, 'b_out': b_out}
    _L1_attn_in = _L1_attn_setup()

    def _L1_ffn_setup():
        import jax, jax.numpy as jnp
        import numpy as np
        DIM = 128
        HIDDEN = 384
        SCALE = 1.0 / 127.0

        def _dequant(w_int, dtype):
            return w_int.astype(dtype) * jnp.asarray(SCALE, dtype)
        key = jax.random.key(seed)
        k_x, k_g, k_u, k_d = jax.random.split(key, 4)
        x = jax.random.normal(k_x, (4, 256, DIM), dtype=jnp.float32)
        w_gate = jax.random.randint(k_g, (HIDDEN, DIM), -127, 128, dtype=jnp.int32)
        w_up = jax.random.randint(k_u, (HIDDEN, DIM), -127, 128, dtype=jnp.int32)
        w_down = jax.random.randint(k_d, (DIM, HIDDEN), -127, 128, dtype=jnp.int32)
        return {'x': x, 'w_gate': w_gate, 'w_up': w_up, 'w_down': w_down}
    _L1_ffn_in = _L1_ffn_setup()

    def _L2_attn_setup():
        import jax, jax.numpy as jnp
        import numpy as np
        EPS = 1e-08
        key = jax.random.key(seed)
        k0, k1, k2, k3 = jax.random.split(key, 4)
        B, S, D = (8, 256, 128)
        scale = 1.0 / np.sqrt(D)
        x = jax.random.normal(k0, (B, S, D), dtype=jnp.float32)
        Wq = jax.random.normal(k1, (D, D), dtype=jnp.float32) * scale
        Wk = jax.random.normal(k2, (D, D), dtype=jnp.float32) * scale
        Wv = jax.random.normal(k3, (D, D), dtype=jnp.float32) * scale
        return {'x': x, 'Wq': Wq, 'Wk': Wk, 'Wv': Wv}
    _L2_attn_in = _L2_attn_setup()

    def _L2_ffn_setup():
        import jax, jax.numpy as jnp
        import numpy as np
        B, S, D, H, E = (4, 256, 128, 16, 4)
        key = jax.random.key(seed)
        ks = jax.random.split(key, 8)
        w = lambda k, shape: jax.random.normal(k, shape, jnp.float32) * 0.02
        return {'x': jax.random.normal(ks[0], (B, S, D), jnp.float32), 'router_w': w(ks[1], (D, E)), 'router_b': jnp.zeros((E,), jnp.float32), 'wq': w(ks[2], (E, D, D)), 'bq': jnp.zeros((E, D), jnp.float32), 'wk': w(ks[3], (E, D, D)), 'bk': jnp.zeros((E, D), jnp.float32), 'wv': w(ks[4], (E, D, D)), 'bv': jnp.zeros((E, D), jnp.float32), 'wo': w(ks[5], (E, D, D)), 'bo': jnp.zeros((E, D), jnp.float32)}
    _L2_ffn_in = _L2_ffn_setup()

    def _L3_attn_setup():
        import jax, jax.numpy as jnp
        import numpy as np
        D_MODEL = 128
        N_HEADS = 16
        HEAD_DIM = D_MODEL // N_HEADS
        SCALE = HEAD_DIM ** (-0.5)

        def apply_rotary(x):
            seq_len = x.shape[-2]
            freqs = 10000.0 ** (jnp.arange(0, HEAD_DIM, 2.0, dtype=jnp.float32) / HEAD_DIM)
            t = jnp.arange(seq_len, dtype=jnp.float32)
            angles = t[:, None] * freqs[None, :]
            sin = jnp.sin(angles)[None, None]
            cos = jnp.cos(angles)[None, None]
            x1, x2 = (x[..., ::2], x[..., 1::2])
            return jnp.concatenate([x1 * cos - x2 * sin, x2 * cos + x1 * sin], axis=-1)
        key = jax.random.key(seed)
        ks = jax.random.split(key, 5)
        B, T = (2, 256)
        std = D_MODEL ** (-0.5)
        return {'x': jax.random.normal(ks[0], (B, T, D_MODEL), dtype=jnp.float32), 'qkv_w': jax.random.normal(ks[1], (D_MODEL, 3 * D_MODEL), dtype=jnp.float32) * std, 'qkv_b': jnp.zeros((3 * D_MODEL,), dtype=jnp.float32), 'out_w': jax.random.normal(ks[2], (D_MODEL, D_MODEL), dtype=jnp.float32) * std, 'out_b': jnp.zeros((D_MODEL,), dtype=jnp.float32)}
    _L3_attn_in = _L3_attn_setup()

    def _L3_ffn_setup():
        import jax, jax.numpy as jnp
        import numpy as np
        import math
        D_IN = 128
        FEATURES = (512, 512, 128)
        BATCH, SEQ = (8, 256)

        def _conn_dense(kernel_bool, x):
            w = jnp.where(kernel_bool, jnp.float32(1.0), jnp.float32(-1.0))
            return x @ w
        key = jax.random.key(seed)
        kx, kk0, kk1, kk2 = jax.random.split(key, 4)
        x = jax.random.normal(kx, (BATCH, SEQ, D_IN), dtype=jnp.float32)
        k0 = jax.random.randint(kk0, (2 * D_IN, FEATURES[0]), 0, 2).astype(jnp.bool_)
        k1 = jax.random.randint(kk1, (FEATURES[0], FEATURES[1]), 0, 2).astype(jnp.bool_)
        k2 = jax.random.randint(kk2, (FEATURES[1], FEATURES[2]), 0, 2).astype(jnp.bool_)
        s0 = jnp.asarray(1.0 / math.sqrt(2 * D_IN), dtype=jnp.float32)
        s1 = jnp.asarray(1.0 / math.sqrt(FEATURES[0]), dtype=jnp.float32)
        s2 = jnp.asarray(1.0 / math.sqrt(FEATURES[1]), dtype=jnp.float32)
        return {'x': x, 'k0': k0, 'k1': k1, 'k2': k2, 's0': s0, 's1': s1, 's2': s2}
    _L3_ffn_in = _L3_ffn_setup()
    _d = {'L0_attn_x': _L0_attn_in['x'], 'L0_attn_W_qkv': _L0_attn_in['W_qkv'], 'L0_attn_b_qkv': _L0_attn_in['b_qkv'], 'L0_attn_W_o': _L0_attn_in['W_o'], 'L0_attn_b_o': _L0_attn_in['b_o'], 'L0_ffn_w_gate': _L0_ffn_in['w_gate'], 'L0_ffn_w_up': _L0_ffn_in['w_up'], 'L0_ffn_w_down': _L0_ffn_in['w_down'], 'L1_attn_W_qkv': _L1_attn_in['W_qkv'], 'L1_attn_b_qkv': _L1_attn_in['b_qkv'], 'L1_attn_W_out': _L1_attn_in['W_out'], 'L1_attn_b_out': _L1_attn_in['b_out'], 'L1_ffn_w_gate': _L1_ffn_in['w_gate'], 'L1_ffn_w_up': _L1_ffn_in['w_up'], 'L1_ffn_w_down': _L1_ffn_in['w_down'], 'L2_attn_Wq': _L2_attn_in['Wq'], 'L2_attn_Wk': _L2_attn_in['Wk'], 'L2_attn_Wv': _L2_attn_in['Wv'], 'L2_ffn_router_w': _L2_ffn_in['router_w'], 'L2_ffn_router_b': _L2_ffn_in['router_b'], 'L2_ffn_wq': _L2_ffn_in['wq'], 'L2_ffn_bq': _L2_ffn_in['bq'], 'L2_ffn_wk': _L2_ffn_in['wk'], 'L2_ffn_bk': _L2_ffn_in['bk'], 'L2_ffn_wv': _L2_ffn_in['wv'], 'L2_ffn_bv': _L2_ffn_in['bv'], 'L2_ffn_wo': _L2_ffn_in['wo'], 'L2_ffn_bo': _L2_ffn_in['bo'], 'L3_attn_qkv_w': _L3_attn_in['qkv_w'], 'L3_attn_qkv_b': _L3_attn_in['qkv_b'], 'L3_attn_out_w': _L3_attn_in['out_w'], 'L3_attn_out_b': _L3_attn_in['out_b'], 'L3_ffn_k0': _L3_ffn_in['k0'], 'L3_ffn_k1': _L3_ffn_in['k1'], 'L3_ffn_k2': _L3_ffn_in['k2'], 'L3_ffn_s0': _L3_ffn_in['s0'], 'L3_ffn_s1': _L3_ffn_in['s1'], 'L3_ffn_s2': _L3_ffn_in['s2']}
    _x0 = _d['L0_attn_x']
    _d['L0_attn_x'] = jax.random.normal(jax.random.fold_in(jax.random.key(seed), 1), (16, 256, 128), dtype=_x0.dtype)
    del _x0
    return _d

def reference(L0_attn_x, L0_attn_W_qkv, L0_attn_b_qkv, L0_attn_W_o, L0_attn_b_o, L0_ffn_w_gate, L0_ffn_w_up, L0_ffn_w_down, L1_attn_W_qkv, L1_attn_b_qkv, L1_attn_W_out, L1_attn_b_out, L1_ffn_w_gate, L1_ffn_w_up, L1_ffn_w_down, L2_attn_Wq, L2_attn_Wk, L2_attn_Wv, L2_ffn_router_w, L2_ffn_router_b, L2_ffn_wq, L2_ffn_bq, L2_ffn_wk, L2_ffn_bk, L2_ffn_wv, L2_ffn_bv, L2_ffn_wo, L2_ffn_bo, L3_attn_qkv_w, L3_attn_qkv_b, L3_attn_out_w, L3_attn_out_b, L3_ffn_k0, L3_ffn_k1, L3_ffn_k2, L3_ffn_s0, L3_ffn_s1, L3_ffn_s2):

    def _L0_attn_ref(x, W_qkv, b_qkv, W_o, b_o):
        import jax, jax.numpy as jnp
        import numpy as np
        D_MODEL = 128
        N_HEADS = 16
        D_HEAD = 64
        B, S = (8, 128)
        EPS = 1.1920929e-07
        normed = x * jax.lax.rsqrt(jnp.mean(x * x, axis=-1, keepdims=True) + EPS)
        qkv = normed @ W_qkv.T + b_qkv
        qkv = qkv.reshape(*qkv.shape[:-1], N_HEADS, D_HEAD, 3)
        q, k, v = (qkv[..., 0], qkv[..., 1], qkv[..., 2])
        scores = jnp.einsum('bqhd,bkhd->bhqk', q, k)
        seq = x.shape[-2]
        causal_mask = jnp.triu(jnp.ones((seq, seq), dtype=bool), k=1)
        scores = jnp.where(causal_mask, -jnp.inf, scores)
        attn = jax.nn.softmax(scores, axis=-2)
        z = jnp.einsum('bhqk,bkhd->bqhd', attn, v)
        z = z.reshape(*z.shape[:-2], N_HEADS * D_HEAD)
        return z @ W_o.T + b_o

    def _L0_ffn_ref(x, w_gate, w_up, w_down):
        import jax, jax.numpy as jnp
        import numpy as np
        DIM = 128
        HIDDEN = 384
        SCALE = 1.0 / 127.0

        def _dequant(w_int, dtype):
            return w_int.astype(dtype) * jnp.asarray(SCALE, dtype)
        wg = _dequant(w_gate, x.dtype)
        wu = _dequant(w_up, x.dtype)
        wd = _dequant(w_down, x.dtype)
        gate = jnp.einsum('bsd,hd->bsh', x, wg)
        up = jnp.einsum('bsd,hd->bsh', x, wu)
        h = jax.nn.silu(gate) * up
        return jnp.einsum('bsh,dh->bsd', h, wd)

    def _L1_attn_ref(x, W_qkv, b_qkv, W_out, b_out):
        import jax, jax.numpy as jnp
        import numpy as np
        from math import sqrt
        EMBED = 128
        HEADS = 16
        B, N, E = x.shape
        H = HEADS
        d = E // H
        qkv = x @ W_qkv + b_qkv
        q, k, v = jnp.split(qkv, 3, axis=2)
        q = q.reshape(B, N, H, d)
        k = k.reshape(B, N, H, d)
        v = v.reshape(B, N, H, d)
        energy = jnp.einsum('bqhe,bkhe->bqhk', q, k)
        attn = jax.nn.softmax(energy, axis=-1) / sqrt(E)
        out = jnp.einsum('bihv,bvhd->bihd', attn, v)
        out = out.reshape(B, N, E)
        return out @ W_out + b_out

    def _L1_ffn_ref(x, w_gate, w_up, w_down):
        import jax, jax.numpy as jnp
        import numpy as np
        DIM = 128
        HIDDEN = 384
        SCALE = 1.0 / 127.0

        def _dequant(w_int, dtype):
            return w_int.astype(dtype) * jnp.asarray(SCALE, dtype)
        wg = _dequant(w_gate, x.dtype)
        wu = _dequant(w_up, x.dtype)
        wd = _dequant(w_down, x.dtype)
        gate = jnp.einsum('bsd,hd->bsh', x, wg)
        up = jnp.einsum('bsd,hd->bsh', x, wu)
        h = jax.nn.silu(gate) * up
        return jnp.einsum('bsh,dh->bsd', h, wd)

    def _L2_attn_ref(x, Wq, Wk, Wv):
        import jax, jax.numpy as jnp
        import numpy as np
        EPS = 1e-08
        D = x.shape[-1]
        q = jnp.einsum('bsd,ed->bse', x, Wq)
        k = jnp.einsum('bsd,ed->bse', x, Wk)
        v = jnp.einsum('bsd,ed->bse', x, Wv)
        fk = jnp.fft.rfft(k, axis=-1)
        fk = fk / (jnp.abs(fk) + EPS)
        fq = jnp.fft.rfft(q, axis=-1)
        fq = fq / (jnp.abs(fq) + EPS)
        fv = jnp.fft.rfft(v, axis=-1)
        fkv = jnp.cumsum(fk * fv, axis=-2)
        values_hat = jnp.fft.irfft(fkv * jnp.conj(fq), n=D, axis=-1)
        return x + values_hat

    def _L2_ffn_ref(x, router_w, router_b, wq, bq, wk, bk, wv, bv, wo, bo):
        import jax, jax.numpy as jnp
        import numpy as np
        B, S, D, H, E = (4, 256, 128, 16, 4)
        b, s, d = x.shape
        e_total = router_w.shape[-1]
        h = H
        hd = d // h
        sm_scale = 0.5
        logits = x @ router_w + router_b
        probs = jax.nn.softmax(logits, axis=-1)
        _, top2 = jax.lax.top_k(probs, 2)
        out = jnp.zeros_like(x)
        bidx = jnp.arange(b)[:, None]
        for e in range(e_total):
            member = (top2 == e).any(-1)
            w_tok = jnp.where(member, probs[..., e], 0.0)
            order = jnp.argsort((~member).astype(jnp.int32), axis=-1, stable=True)
            xg = jnp.take_along_axis(x, order[..., None], axis=1)
            validg = jnp.take_along_axis(member, order, axis=1)
            wg = jnp.take_along_axis(w_tok, order, axis=1)
            q = (xg @ wq[e] + bq[e]).reshape(b, s, h, hd)
            k = (xg @ wk[e] + bk[e]).reshape(b, s, h, hd)
            v = (xg @ wv[e] + bv[e]).reshape(b, s, h, hd)
            att = jnp.einsum('bqhd,bkhd->bhqk', q, k) * sm_scale
            att = jnp.where(validg[:, None, None, :], att, -1000000000.0)
            att = jax.nn.softmax(att, axis=-1)
            y = jnp.einsum('bhqk,bkhd->bqhd', att, v).reshape(b, s, d)
            y = y @ wo[e] + bo[e]
            out = out.at[bidx, order].add(wg[..., None] * y)
        return out

    def _L3_attn_ref(x, qkv_w, qkv_b, out_w, out_b):
        import jax, jax.numpy as jnp
        import numpy as np
        D_MODEL = 128
        N_HEADS = 16
        HEAD_DIM = D_MODEL // N_HEADS
        SCALE = HEAD_DIM ** (-0.5)

        def apply_rotary(x):
            seq_len = x.shape[-2]
            freqs = 10000.0 ** (jnp.arange(0, HEAD_DIM, 2.0, dtype=jnp.float32) / HEAD_DIM)
            t = jnp.arange(seq_len, dtype=jnp.float32)
            angles = t[:, None] * freqs[None, :]
            sin = jnp.sin(angles)[None, None]
            cos = jnp.cos(angles)[None, None]
            x1, x2 = (x[..., ::2], x[..., 1::2])
            return jnp.concatenate([x1 * cos - x2 * sin, x2 * cos + x1 * sin], axis=-1)
        B, T, D = x.shape
        qkv = x @ qkv_w + qkv_b
        q, k, v = jnp.split(qkv, 3, axis=-1)

        def to_heads(a):
            return a.reshape(B, T, N_HEADS, HEAD_DIM).transpose(0, 2, 1, 3)
        q, k, v = (to_heads(q), to_heads(k), to_heads(v))
        q = apply_rotary(q)
        k = apply_rotary(k)
        scores = jnp.einsum('bhqd,bhkd->bhqk', q, k) * SCALE
        weights = jax.nn.softmax(scores, axis=-1)
        attn = jnp.einsum('bhqk,bhkd->bhqd', weights, v)
        attn = attn.transpose(0, 2, 1, 3).reshape(B, T, D)
        return attn @ out_w + out_b

    def _L3_ffn_ref(x, k0, k1, k2, s0, s1, s2):
        import jax, jax.numpy as jnp
        import numpy as np
        import math
        D_IN = 128
        FEATURES = (512, 512, 128)
        BATCH, SEQ = (8, 256)

        def _conn_dense(kernel_bool, x):
            w = jnp.where(kernel_bool, jnp.float32(1.0), jnp.float32(-1.0))
            return x @ w
        h = jnp.concatenate([x, -x], axis=-1)
        h = s0 * _conn_dense(k0, h)
        h = jax.nn.relu(h) * 2
        h = s1 * _conn_dense(k1, h)
        h = jax.nn.relu(h) * 2
        h = s2 * _conn_dense(k2, h)
        return h
    x = L0_attn_x
    x = x + _L0_attn_ref(_layernorm(x, axis=-1), L0_attn_W_qkv, L0_attn_b_qkv, L0_attn_W_o, L0_attn_b_o)
    x = x + _L0_ffn_ref(_layernorm(x, axis=-1), L0_ffn_w_gate, L0_ffn_w_up, L0_ffn_w_down)
    x = x + _L1_attn_ref(_layernorm(x, axis=-1), L1_attn_W_qkv, L1_attn_b_qkv, L1_attn_W_out, L1_attn_b_out)
    x = x + _L1_ffn_ref(_layernorm(x, axis=-1), L1_ffn_w_gate, L1_ffn_w_up, L1_ffn_w_down)
    x = x + _L2_attn_ref(_layernorm(x, axis=-1), L2_attn_Wq, L2_attn_Wk, L2_attn_Wv)
    x = x + _L2_ffn_ref(_layernorm(x, axis=-1), L2_ffn_router_w, L2_ffn_router_b, L2_ffn_wq, L2_ffn_bq, L2_ffn_wk, L2_ffn_bk, L2_ffn_wv, L2_ffn_bv, L2_ffn_wo, L2_ffn_bo)
    x = x + _L3_attn_ref(_layernorm(x, axis=-1), L3_attn_qkv_w, L3_attn_qkv_b, L3_attn_out_w, L3_attn_out_b)
    x = x + _L3_ffn_ref(_layernorm(x, axis=-1), L3_ffn_k0, L3_ffn_k1, L3_ffn_k2, L3_ffn_s0, L3_ffn_s1, L3_ffn_s2)
    return x

_drawn_inputs = setup_inputs


def setup_inputs(seed=0):
    import zlib

    import numpy as np

    out = dict(_drawn_inputs(seed))
    spreads = {'L0_attn_b_qkv': (0.0, 0.1),
     'L0_attn_b_o': (0.0, 0.1),
     'L2_ffn_router_b': (0.0, 2.0),
     'L2_ffn_bq': (0.0, 2.0),
     'L2_ffn_bk': (0.0, 0.8),
     'L2_ffn_bv': (0.0, 2.0),
     'L2_ffn_bo': (0.0, 2.0),
     'L3_attn_qkv_b': (0.0, 0.8),
     'L3_attn_out_b': (0.0, 2.0)}
    factors = {'L1_attn_W_qkv': 8.0,
     'L1_attn_b_qkv': 64.0,
     'L1_attn_W_out': 8.0,
     'L1_attn_b_out': 64.0,
     'L2_ffn_router_w': 64.0,
     'L2_ffn_wq': 64.0,
     'L2_ffn_wk': 64.0,
     'L2_ffn_wv': 64.0,
     'L2_ffn_wo': 62.827,
     'L3_attn_qkv_w': 8.0,
     'L3_attn_out_w': 8.0}
    for name, (base, spread) in spreads.items():
        noise = np.random.default_rng([zlib.crc32(name.encode()), seed]).standard_normal(out[name].shape)
        drawn = base * np.exp(spread * noise) if base else spread * noise
        out[name] = jnp.asarray(drawn.astype(out[name].dtype))
    for name, factor in factors.items():
        out[name] = (out[name] * factor).astype(out[name].dtype)
    return out
```

```python
from contextlib import ExitStack

import numpy as np

import concourse.bass as bass
from concourse import mybir

F32 = mybir.dt.float32
BF16 = mybir.dt.bfloat16
I32 = mybir.dt.int32
U8 = mybir.dt.uint8
ALU = mybir.AluOpType
ACT = mybir.ActivationFunctionType
AX_X = mybir.AxisListType.X

P = 128
D = 128
BATCHES = 16
SEQ = 256
TILES = BATCHES * SEQ // P
GROUPS = 8
LN_EPS = 1e-5

HEADS = 16
HD = 8
SLOT = 32
BF_ROWS = 48
MASK_ROW = 64
MAX_ROW = 96
EXPERTS = 4

L0_HEADS = 16
L0_HD = 64
L0_PAIRS = L0_HEADS // 2
RMS_EPS = 1.1920929e-07

FREQS = D // 2 + 1
HIDDEN = 384
HCH = HIDDEN // P
FF3 = 512
NEG = -1e30


class Plan:

    def __init__(self, jobs, weights, unroll, first, rounds, drain, misc_uses=()):
        self.jobs, self.weights, self.unroll, self.first = jobs, weights, unroll, first
        self.rounds, self.drain, self.misc_uses = rounds, drain, misc_uses


class Weights:

    def __init__(self, wq=None, wk=None, wv=None, wo=None, bq=None, bk=None, bqk=None, bv=None, bo=None, wq2=None, wk2=None,
                 rot_bias=None, tables=None, router=None, router_b=None, qscale=1.0, ones_value=1.0,
                 gate=None, up=None, down=None, kqv=None, back=None, k0=None, k1=None, k2=None, s=None):
        self.wq, self.wk, self.wv, self.wo, self.bq, self.bk, self.bqk, self.bv, self.bo = wq, wk, wv, wo, bq, bk, bqk, bv, bo
        self.wq2, self.wk2, self.rot_bias, self.tables = wq2, wk2, rot_bias, tables
        self.router, self.router_b, self.qscale, self.ones_value = router, router_b, qscale, ones_value
        self.gate, self.up, self.down, self.kqv, self.back = gate, up, down, kqv, back
        self.k0, self.k1, self.k2, self.s = k0, k1, k2, s


class Model:

    def __init__(self, ctx):
        self.ctx = ctx


def stage(nc, ctx, name):
    held = []

    def sem(n):
        held.append(ctx.enter_context(nc.semaphore(f"{name}_{n}")))
        return held[-1]

    def sb(n, shape, dt=F32):
        return ctx.enter_context(nc.sbuf_tensor(f"{name}_{n}", shape, dt))

    def clear():
        with nc.Block() as block:
            @block.sync
            def _(sp):
                for h in held:
                    sp.sem_clear(h)

    def begin():
        ctx.callback(clear)
        return ctx.enter_context(nc.Block())

    return sem, sb, begin


def layer_norm(nc, m, name, rms=False, add_to_x=False):
    with ExitStack() as ctx:
        sem, sb, begin = stage(nc, ctx, name)
        stats = sb("stats", [P, TILES, 6])
        small = sb("small", [P, 8, TILES])
        xn = sb("xn", [P, 2, 4, D])
        turned = [ctx.enter_context(nc.psum_tensor(f"{name}_turned{k}", [P, 512], F32)) for k in range(2)]
        by_group = lambda a: a.rearrange("p (g k) -> p g k", k=4)
        mean, dif, var, root, rstd, tmp, guarded, shift = (small[:, k, :] for k in range(8))
        stats_done, dve_step, guarded_ready, root_ready = sem("stats_done"), sem("dve_step"), sem("guarded_ready"), sem("root_ready")
        xn_ready, turned_ready, xT_written, x_added = sem("xn_ready"), sem("turned_ready"), sem("xT_written"), sem("x_added")
        block = begin()

        @block.vector
        def _(dve):
            with dve.Fori(0, GROUPS) as g:
                for k in range(4):
                    dve.bn_stats(stats[:, :, :].rearrange("p (g k) c -> p g k c", k=4)[:, g, k, :], m.x4[:, g, k, :]).then_inc(stats_done, 1)
            dve.wait_ge(stats_done, TILES)
            n = [0]

            def then_wait(ins):
                n[0] += 1
                ins.then_inc(dve_step, 1)
                dve.wait_ge(dve_step, n[0])

            even, odd = stats[:, :, 1], stats[:, :, 4]
            dve.tensor_tensor(dif, even, odd, ALU.subtract).then_inc(dve_step, 1)
            dve.tensor_tensor(mean, even, odd, ALU.add).then_inc(dve_step, 1)
            n[0] = 2
            dve.wait_ge(dve_step, 2)
            dve.tensor_tensor(tmp, dif, dif, ALU.mult).then_inc(dve_step, 1)
            n[0] = 3
            then_wait(dve.tensor_tensor(var, stats[:, :, 2], stats[:, :, 5], ALU.add))
            then_wait(dve.scalar_tensor_tensor(out=var, in0=tmp, scalar=float(D // 4), in1=var, op0=ALU.mult, op1=ALU.add))
            if rms:
                then_wait(dve.tensor_scalar(guarded, var, (1.0 + RMS_EPS) / D, RMS_EPS * LN_EPS, ALU.mult, ALU.add))
            else:
                then_wait(dve.tensor_scalar(guarded, var, 1.0 / D, LN_EPS, ALU.mult, ALU.add))
            dve.tensor_scalar(mean, mean, 0.5, None, ALU.mult).then_inc(guarded_ready, 1)
            dve.wait_ge(guarded_ready, 1)
            dve.wait_ge(root_ready, 1)
            then_wait(dve.reciprocal(rstd, root))
            then_wait(dve.tensor_tensor(tmp, rstd, rstd, ALU.mult))
            then_wait(dve.tensor_tensor(tmp, tmp, guarded, ALU.mult))
            then_wait(dve.tensor_scalar(tmp, tmp, -0.5, 1.5, ALU.mult, ALU.add))
            then_wait(dve.tensor_tensor(rstd, rstd, tmp, ALU.mult))
            with dve.Fori(0, GROUPS // 2) as r:
                for b in range(2):
                    g = r * 2 + b
                    dve.wait_ge(turned_ready, r * 2 + b)
                    if add_to_x:
                        dve.wait_ge(x_added, r * 8 + b * 4)
                    for k in range(4):
                        dve.tensor_scalar(xn[:, b, k, :], m.x4[:, g, k, :], by_group(mean)[:, g, k:k + 1], by_group(rstd)[:, g, k:k + 1],
                                          ALU.subtract, ALU.mult).then_inc(xn_ready, 1)
                    if add_to_x:
                        dve.wait_ge(xn_ready, r * 8 + b * 4 + 4)
                        for k in range(4):
                            dve.tensor_tensor(m.x4[:, g, k, :], m.x4[:, g, k, :], xn[:, b, k, :], ALU.add).then_inc(x_added, 1)

        @block.scalar
        def _(act):
            act.wait_ge(dve_step, 6)
            act.activation(root, guarded, ACT.Sqrt).then_inc(root_ready, 1)
            with act.Fori(0, GROUPS // 2) as r:
                for b in range(2):
                    act.wait_ge(turned_ready, r * 2 + b + 1)
                    act.activation(m.xT8[:, r * 2 + b, :], turned[b][:, :], ACT.Copy).then_inc(xT_written, 1)

        @block.tensor
        def _(pe):
            with pe.Fori(0, GROUPS // 2) as r:
                for b in range(2):
                    pe.wait_ge(xn_ready, r * 8 + b * 4 + 4)
                    pe.wait_ge(xT_written, r * 2 + b)
                    for k in range(4):
                        t = pe.transpose(turned[b][:, k * D:(k + 1) * D], xn[:, b, k, :], m.identity[:, :])
                    t.then_inc(turned_ready, 1)


class Step:

    def __init__(self, plan, at, turns):
        self.plan, self.at = plan, at
        self.turns = turns
        self.past = turns * plan.unroll if turns is not None else 0

    def has(self, off):
        return 0 <= self.at + off < self.plan.jobs

    def known(self, off, least=0):
        return self.at + off >= least

    def n(self, off, per=1, plus=0):
        return self.past * per + ((self.at + off) * per + plus)

    def parity(self, off):
        return (self.at + off) % 2

    def expert(self, off):
        return (self.at + off) % self.plan.weights

    def batch(self, off):
        b = (self.at + off) // self.plan.weights
        return b if self.turns is None else self.turns * (self.plan.unroll // self.plan.weights) + b

    def use(self, kind, off):
        uses = self.plan.misc_uses
        kinds = [k for k, _ in uses]
        mine = kinds.index(kind)
        step = self.at + off - uses[mine][1]
        n = sum(0 <= at + o < self.plan.jobs for at in range(-3, step) for _, o in uses)
        n += sum(0 <= step + o < self.plan.jobs for _, o in uses[:mine + 1])
        return self.past * len(uses) + n


def wait_alone(engine, sem, value, passed):
    engine.wait_ge(sem, value)
    engine.sem_inc(passed, 1)


def pipeline(engine, plan, step):
    for at in range(-3, plan.first):
        step(Step(plan, at, None))
    with engine.Fori(0, plan.rounds) as turns:
        for u in range(plan.unroll):
            step(Step(plan, plan.first + u, turns))
    for at in range(plan.first + plan.rounds * plan.unroll, plan.jobs + plan.drain):
        step(Step(plan, at, None))


def attention8(nc, m, name, w, weights=1, rotary=False, masked=False):
    jobs, unroll, first = BATCHES * weights, max(2, weights), 4
    plan = Plan(jobs, weights, unroll, first, rounds=(jobs - 3 - first) // unroll, drain=1)
    plan.misc_uses = ([("qk", 2)] + [("o2", -1)] + ([("qk2", 2)] if rotary else []) +
                      [("m1", 0), ("o3", -1), ("v", 1), ("y", -1), ("o0", 0), ("out", -1), ("m0", 1), ("o1", 0)])

    with ExitStack() as ctx:
        sem, sb, begin = stage(nc, ctx, name)
        xcur = sb("xcur", [P, 2, SEQ])
        qk32 = sb("qk32", [P, 2, SEQ])
        rest = sb("rest", [P, 2, SEQ])
        parts = sb("parts", [P, 2, 3, SEQ], BF16)
        stackq = sb("stackq", [P, 2, HEADS, SEQ], BF16)
        stackk = sb("stackk", [P, 2, HEADS, SEQ], BF16)
        values = sb("values", [P, 2, 2, HEADS, SLOT])
        probs = sb("probs", [P, 2, 4, 2 * SEQ])
        rowmax = sb("rowmax", [P, 2, HEADS, 2])
        maxdif = sb("maxdif", [P, 2, 2, 8])
        negmax = sb("negmax", [P, 2, 2, 2, 8], BF16)
        negmaxT = sb("negmaxT", [16, 2, SEQ], BF16)
        oT = sb("oT", [P, 2, SEQ])
        rden = sb("rden", [P, 2, 2, 4])
        y = sb("y", [P, 2, D])
        yT = sb("yT", [P, SEQ])
        if rotary:
            turned = sb("turned", [P, 2, 2, SEQ])
        psS = [ctx.enter_context(nc.psum_tensor(f"{name}_psS{k}", [P, 512], F32)) for k in range(2)]
        psT = [ctx.enter_context(nc.psum_tensor(f"{name}_psT{k}", [P, 1024], F32)) for k in range(2)]
        psO = ctx.enter_context(nc.psum_tensor(f"{name}_psO", [P, 512], F32))
        psM = ctx.enter_context(nc.psum_tensor(f"{name}_psM", [P, 512], F32))
        scratch = nc.dram_tensor(f"{name}_scratch", (2, 2, 3, P, SEQ), BF16, kind="Internal").ap()

        preset, zeros, stacks_zero, tokens_ready = sem("preset"), sem("zeros"), sem("stacks_zero"), sem("tokens_ready")
        sp_passed, pool_passed = sem("sp_passed"), sem("pool_passed")
        misc_full, misc_taken = sem("misc_full"), sem("misc_taken")
        split_step, parts_ready, parts_saved = sem("split_step"), sem("parts_ready"), sem("parts_saved")
        stack_ready = [sem("stack_ready0"), sem("stack_ready1")]
        scores_ready, max_done = sem("scores_ready"), sem("max_done")
        negmax_step, negmax_ready = sem("negmax_step"), sem("negmax_ready")
        maxrow_ready = [sem("maxrow_ready0"), sem("maxrow_ready1")]
        shifted_ready, exp_done = sem("shifted_ready"), sem("exp_done")
        pv_ready, oT_ready, rden_ready = sem("pv_ready"), sem("oT_ready"), sem("rden_ready")
        splits = 4 if rotary else 3
        stack_inc = 16 * (6 + (1 if masked else 0))

        block = begin()

        @block.sync
        def _(sp):
            sp.wait_ge(preset, 3)

            def max_rows(s, off, half):
                wait_alone(sp, misc_taken, s.use(f"m{half}", off), sp_passed)
                for part in range(2):
                    sp.dma_start(stackq[MAX_ROW + part:MAX_ROW + part + 1, s.parity(off), 8 * half:8 * half + 8, :],
                                 negmaxT[8 * part:8 * part + 8, half, :]).then_inc(maxrow_ready[half], 16)

            def stack(s, half):
                b = s.parity(2)
                hs = slice(8 * half, 8 * half + 8)
                src = scratch[b].rearrange("qk part (d h) t -> qk part d h t", h=HEADS)
                for repeats, part, row in ((3, 0, 0), (2, 1, 24), (1, 2, 40)):
                    rows = slice(row, row + 8 * repeats)
                    sp.dma_start(stackq[rows, b, hs, :], src[0, part, :, hs, :].unsqueeze(0).to_broadcast([repeats, HD, 8, SEQ])).then_inc(stack_ready[half], 16)
                    sp.dma_start(stackk[rows, b, hs, :], src[1, 0:repeats, :, hs, :]).then_inc(stack_ready[half], 16)
                if masked:
                    row = m.mask_dram[s.batch(2), s.expert(2)]
                    sp.dma_start(stackk[MASK_ROW:MASK_ROW + 1, b, hs, :],
                                 row.unsqueeze(0).unsqueeze(0).to_broadcast([1, 8, SEQ])).then_inc(stack_ready[half], 16)

            def step(s):
                if s.has(0):
                    max_rows(s, 0, 1)
                if s.has(2):
                    wait_alone(sp, parts_ready, s.n(2, 1, 1), sp_passed)
                    if s.known(2, 2):
                        wait_alone(sp, stack_ready[1], s.n(2, stack_inc, -stack_inc), sp_passed)
                    sp.dma_start(scratch[s.parity(2)].rearrange("qk part p t -> p qk part t"),
                                 parts[:, :, :, :]).then_inc(parts_saved, 16)
                    wait_alone(sp, parts_saved, s.n(2, 16, 16), sp_passed)
                    if s.known(2, 2):
                        wait_alone(sp, shifted_ready, s.n(0, 8, 4), sp_passed)
                    stack(s, 0)
                if s.has(1):
                    max_rows(s, 1, 0)
                if s.has(2):
                    if s.known(2, 2):
                        wait_alone(sp, shifted_ready, s.n(0, 8, 8), sp_passed)
                    stack(s, 1)

            pipeline(sp, plan, step)

        @block.tensor
        def _(pe):
            pe.wait_ge(preset, 3)

            def misc_use(s, kind, off):
                pe.wait_ge(misc_taken, s.use(kind, off) - 1)

            def project_qk(s, kind, wq, wk):
                pe.wait_ge(tokens_ready, s.n(2, 1, 1))
                misc_use(s, kind, 2)
                xc = xcur[:, s.parity(2), :]
                pe.matmul(psM[:, 0:SEQ], wq[:, s.expert(2), :], xc, start=True, stop=True)
                pe.matmul(psM[:, SEQ:2 * SEQ], wk[:, s.expert(2), :], xc, start=True, stop=True).then_inc(misc_full, 1)

            def project_v(s):
                misc_use(s, "v", 1)
                for t in range(2):
                    mm = pe.matmul(psM[:, t * D:(t + 1) * D], xcur[:, s.parity(1), t * P:(t + 1) * P],
                                   w.wv[:, s.expert(1), :], start=True, stop=True)
                mm.then_inc(misc_full, 1)

            def scores(s, h):
                if h % 8 == 0:
                    pe.wait_ge(stack_ready[h // 8], s.n(1, stack_inc, stack_inc))
                if s.known(1, 1) or h >= 2:
                    pe.wait_ge(max_done, s.n(1, HEADS, h - 1))
                b = s.parity(1)
                for t in range(2):
                    mm = pe.matmul(psS[h % 2][:, t * SEQ:(t + 1) * SEQ], stackq[0:MASK_ROW + 1, b, h, t * P:(t + 1) * P],
                                   stackk[0:MASK_ROW + 1, b, h, :], start=True, stop=True)
                mm.then_inc(scores_ready, 1)

            def shifted(s, h):
                if h % 8 == 0:
                    pe.wait_ge(maxrow_ready[h // 8], s.n(0, 32, 32))
                if h % 2 == 0 and (s.known(0, 1) or h >= 4):
                    pe.wait_ge(exp_done, s.n(0, HEADS // 2, h // 2 - 1))
                b = s.parity(0)
                for t in range(2):
                    mm = pe.matmul(psT[h // 2 % 2][:, (h % 2) * 512 + t * SEQ:(h % 2) * 512 + (t + 1) * SEQ],
                                   stackk[0:MAX_ROW + 2, b, h, t * P:(t + 1) * P],
                                   stackq[0:MAX_ROW + 2, b, h, :], start=True, stop=True)
                if h % 2:
                    mm.then_inc(shifted_ready, 1)

            def prob_values(s, off, g):
                if g == 0:
                    pe.wait_ge(misc_taken, s.use("v", off))
                pe.wait_ge(exp_done, s.n(off, HEADS // 2, 2 * g + 2))
                if s.known(off, 1) or g:
                    pe.wait_ge(oT_ready, s.n(off, 4, g))
                for t in range(2):
                    for j in range(4):
                        mm = pe.matmul(psO[SLOT * j:SLOT * (j + 1), 0:SEQ], values[:, s.parity(off), t, 4 * g + j, :],
                                       probs[:, g % 2, j, t * SEQ:(t + 1) * SEQ], start=(t == 0), stop=(t == 1),
                                       tile_position=(0, SLOT * j), skip_group_check=True)
                mm.then_inc(pv_ready, 1)

            def turn_output(s, off, g):
                pe.wait_ge(oT_ready, s.n(off, 4, g + 1))
                misc_use(s, f"o{g}", off)
                for t in range(2):
                    mm = pe.transpose(psM[:, t * P:(t + 1) * P], oT[:, g % 2, t * P:(t + 1) * P], m.identity[:, :])
                mm.then_inc(misc_full, 1)

            def turn_max(s, off, half):
                pe.wait_ge(negmax_ready, s.n(off, 2, half + 1))
                misc_use(s, f"m{half}", off)
                for t in range(2):
                    mm = pe.transpose(psM[0:16, 0:P].bitcast(BF16)[:, t * P:(t + 1) * P],
                                      negmax[:, half, t, :, :].rearrange("p a h -> p (a h)"), m.identity_bf[:, :])
                mm.then_inc(misc_full, 1)

            def turn_y(s):
                misc_use(s, "y", -1)
                for t in range(2):
                    mm = pe.transpose(psM[:, t * P:(t + 1) * P], y[:, t, :], m.identity[:, :])
                mm.then_inc(misc_full, 1)

            def project_out(s):
                misc_use(s, "out", -1)
                e = s.expert(-1)
                for t in range(2):
                    pe.matmul(psM[:, t * D:(t + 1) * D], yT[:, t * P:(t + 1) * P], w.wo[:, e, :], start=True, stop=False)
                    mm = pe.matmul(psM[:, t * D:(t + 1) * D], m.ones[:, :], w.bo[:, e, :], start=False, stop=True)
                mm.then_inc(misc_full, 1)

            def step(s):
                for h in range(HEADS):
                    if s.has(1):
                        scores(s, h)
                    if s.has(0):
                        shifted(s, h)
                    if h == 0 and s.has(2):
                        project_qk(s, "qk", w.wq, w.wk)
                    if h == 1 and s.has(-1):
                        turn_output(s, -1, 2)
                    if h == 2 and s.has(-1):
                        prob_values(s, -1, 3)
                    if h == 3 and rotary and s.has(2):
                        project_qk(s, "qk2", w.wq2, w.wk2)
                    if h == 4 and s.has(0):
                        turn_max(s, 0, 1)
                    if h == 5 and s.has(-1):
                        turn_output(s, -1, 3)
                    if h in (6, 10, 14) and s.has(0):
                        prob_values(s, 0, (h - 6) // 4)
                    if h == 7 and s.has(1):
                        project_v(s)
                    if h == 8 and s.has(-1):
                        turn_y(s)
                    if h == 9 and s.has(0):
                        turn_output(s, 0, 0)
                    if h == 11 and s.has(-1):
                        project_out(s)
                    if h == 12 and s.has(1):
                        turn_max(s, 1, 0)
                    if h == 13 and s.has(0):
                        turn_output(s, 0, 1)

            pipeline(pe, plan, step)

        @block.scalar
        def _(act):
            def qk_bias(s):
                act.wait_ge(misc_full, s.use("qk", 2))
                if s.known(2, 1):
                    act.wait_ge(parts_ready, s.n(2))
                e = s.expert(2)
                act.activation(qk32[:, 0, :], psM[:, 0:SEQ], ACT.Identity, bias=w.bq[:, e:e + 1], scale=w.qscale)
                act.activation(qk32[:, 1, :], psM[:, SEQ:2 * SEQ], ACT.Identity, bias=w.bk[:, e:e + 1]).then_inc(misc_taken, 1)

            def exponential(s, k):
                act.wait_ge(shifted_ready, s.n(0, 8, k + 1))
                if k % 2 == 0 and (s.known(0, 1) or k >= 4):
                    act.wait_ge(pv_ready, s.n(0, 4, k // 2 - 1))
                act.activation(probs[:, k // 2 % 2, 2 * (k % 2):2 * (k % 2) + 2, :], psT[k % 2][:, :], ACT.Exp).then_inc(exp_done, 1)

            def copy_oT(s, off, g):
                act.wait_ge(pv_ready, s.n(off, 4, g + 1))
                if g >= 2:
                    act.wait_ge(misc_taken, s.use(f"o{g - 2}", off))
                elif s.known(off, 1):
                    act.wait_ge(misc_taken, s.use(f"o{g + 2}", off - 1))
                act.activation(oT[:, g % 2, :], psO[:, 0:SEQ], ACT.Copy).then_inc(oT_ready, 1)

            def copy_max(s, off, half):
                act.wait_ge(misc_full, s.use(f"m{half}", off))
                if s.known(off, 1):
                    act.wait_ge(maxrow_ready[half], s.n(off, 32))
                act.activation(negmaxT[:, half, :], psM[0:16, 0:P].bitcast(BF16), ACT.Copy).then_inc(misc_taken, 1)

            def copy_yT(s):
                act.wait_ge(misc_full, s.use("y", -1))
                if s.known(-1, 1):
                    act.wait_ge(misc_taken, s.use("out", -2))
                act.activation(yT[:, :], psM[:, 0:SEQ], ACT.Copy).then_inc(misc_taken, 1)

            def step(s):
                for h in range(HEADS):
                    if h == 0 and s.has(2) and not rotary:
                        qk_bias(s)
                    if h == 3 and s.has(-1):
                        copy_oT(s, -1, 3)
                    if h == 4 and s.has(0):
                        copy_max(s, 0, 1)
                    if h == 8 and s.has(-1):
                        copy_yT(s)
                    if h == 12 and s.has(1):
                        copy_max(s, 1, 0)
                    if h % 2 and s.has(0):
                        exponential(s, h // 2)
                    if h in (7, 11, 15) and s.has(0):
                        copy_oT(s, 0, (h - 7) // 4)

            pipeline(act, plan, step)

        @block.vector
        def _(dve):
            dve.memset(values[:, :, :, :, :], 0.0).then_inc(zeros, 1)
            dve.wait_ge(zeros, 1)
            dve.memset(values[:, :, :, :, HD:HD + 1], w.ones_value).then_inc(preset, 1)
            dve.wait_ge(stacks_zero, 2)
            dve.memset(stackq[MASK_ROW:MASK_ROW + 1, :, :, :], 1.0).then_inc(preset, 1)
            dve.memset(stackk[MAX_ROW:MAX_ROW + 2, :, :, :], 1.0).then_inc(preset, 1)

            def rotary_half(s, kind, which):
                dve.wait_ge(misc_full, s.use(kind, 2))
                if which == 0 and s.known(2, 1):
                    dve.wait_ge(split_step, s.n(2, splits))
                for k in range(2):
                    t = dve.scalar_tensor_tensor(out=turned[:, which, k, :], in0=psM[:, k * SEQ:(k + 1) * SEQ],
                                                 scalar=w.rot_bias[:, 2 * which + k:2 * which + k + 1], in1=w.tables[:, which, k, :],
                                                 op0=ALU.add, op1=ALU.mult)
                t.then_inc(misc_taken, 1)

            def maxima(s, h):
                dve.wait_ge(scores_ready, s.n(1, HEADS, h + 1))
                if h % 8 == 0 and s.known(1, 2):
                    dve.wait_ge(negmax_ready, s.n(1, 2, h // 8 - 3))
                dve.tensor_reduce(rowmax[:, s.parity(1), h, :], psS[h % 2][:, :].rearrange("p (t k) -> p t k", t=2),
                                  AX_X, ALU.max).then_inc(max_done, 1)

            def write_values(s):
                dve.wait_ge(misc_full, s.use("v", 1))
                if s.known(1, 2):
                    dve.wait_ge(pv_ready, s.n(1, 4, -4))
                dve.tensor_tensor(values[:, s.parity(1), :, :, 0:HD], psM[:, 0:2 * D].rearrange("p (t h d) -> p t h d", t=2, d=HD),
                                  w.bv[:, s.expert(1), :].rearrange("p (h d) -> p h d", d=HD).unsqueeze(1).to_broadcast([P, 2, HEADS, HD]),
                                  ALU.add).then_inc(misc_taken, 1)

            def normalise(s, off, g):
                dve.wait_ge(misc_full, s.use(f"o{g}", off))
                if g == 0 and s.known(off, 1):
                    dve.wait_ge(misc_taken, s.use("y", off - 1))
                o = psM[:, 0:SEQ].rearrange("p (t j c) -> p t j c", t=2, c=SLOT)
                dve.reciprocal(rden[:, g % 2, :, :], o[:, :, :, HD]).then_inc(rden_ready, 1)
                dve.wait_ge(rden_ready, s.n(off, 4, g + 1))
                dve.tensor_tensor(y[:, :, 4 * HD * g:4 * HD * (g + 1)].rearrange("p t (j d) -> p t j d", d=HD), o[:, :, :, 0:HD],
                                  rden[:, g % 2, :, :].unsqueeze(3).to_broadcast([P, 2, 4, HD]), ALU.mult).then_inc(misc_taken, 1)

            def add_output(s):
                dve.wait_ge(misc_full, s.use("out", -1))
                if s.known(-1, 1):
                    dve.wait_ge(misc_taken, s.use("out", -2))
                b, e = s.batch(-1), s.expert(-1)
                if masked:
                    for t in range(2):
                        u = dve.scalar_tensor_tensor(out=m.x32[:, b, t, :], in0=psM[:, t * D:(t + 1) * D],
                                                     scalar=m.gate[:, b, t, e:e + 1], in1=m.x32[:, b, t, :],
                                                     op0=ALU.mult, op1=ALU.add)
                else:
                    u = dve.tensor_tensor(m.x16[:, b, :], psM[:, 0:SEQ], m.x16[:, b, :], ALU.add)
                u.then_inc(misc_taken, 1)

            def step(s):
                for h in range(HEADS):
                    if s.has(1):
                        maxima(s, h)
                    if h == 0 and rotary and s.has(2):
                        rotary_half(s, "qk", 0)
                    if h == 2 and s.has(-1):
                        normalise(s, -1, 2)
                    if h == 3 and rotary and s.has(2):
                        rotary_half(s, "qk2", 1)
                    if h == 6 and s.has(-1):
                        normalise(s, -1, 3)
                    if h == 8 and s.has(1):
                        write_values(s)
                    if h == 10 and s.has(0):
                        normalise(s, 0, 0)
                    if h == 12 and s.has(-1):
                        add_output(s)
                    if h == 14 and s.has(0):
                        normalise(s, 0, 1)

            pipeline(dve, plan, step)

        @block.gpsimd
        def _(pool):
            pool.memset(stackq[:, :, :, :], 0.0).then_inc(stacks_zero, 1)
            pool.memset(stackk[:, :, :, :], 0.0).then_inc(stacks_zero, 1)

            def tokens(s):
                if s.known(3, 2):
                    wait_alone(pool, misc_taken, s.use("v", 1), pool_passed)
                pool.tensor_copy(xcur[:, s.parity(3), :], m.xT16[:, s.batch(3), :]).then_inc(tokens_ready, 1)

            def split(s):
                done = splits - 3
                if rotary:
                    wait_alone(pool, misc_taken, s.use("qk2", 2), pool_passed)
                    pool.tensor_tensor(qk32[:, :, :], turned[:, 0, :, :], turned[:, 1, :, :], ALU.add).then_inc(split_step, 1)
                    wait_alone(pool, split_step, s.n(2, splits, 1), pool_passed)
                else:
                    wait_alone(pool, misc_taken, s.use("qk", 2), pool_passed)
                if s.known(2, 1):
                    wait_alone(pool, parts_saved, s.n(2, 16), pool_passed)
                pool.tensor_copy(parts[:, :, 0, :], qk32[:, :, :]).then_inc(split_step, 1)
                wait_alone(pool, split_step, s.n(2, splits, done + 1), pool_passed)
                pool.tensor_tensor(rest[:, :, :], qk32[:, :, :], parts[:, :, 0, :], ALU.subtract).then_inc(split_step, 1)
                wait_alone(pool, split_step, s.n(2, splits, done + 2), pool_passed)
                pool.tensor_copy(parts[:, :, 1, :], rest[:, :, :]).then_inc(split_step, 1)
                wait_alone(pool, split_step, s.n(2, splits, done + 3), pool_passed)
                pool.tensor_tensor(parts[:, :, 2, :], rest[:, :, :], parts[:, :, 1, :], ALU.subtract).then_inc(parts_ready, 1)

            def split_max(s, half):
                wait_alone(pool, max_done, s.n(1, HEADS, 8 * half + 8), pool_passed)
                if s.known(1, 1):
                    wait_alone(pool, misc_taken, s.use(f"m{half}", 0), pool_passed)
                mx = rowmax[:, s.parity(1), 8 * half:8 * half + 8, :].rearrange("p h t -> p t h")
                pool.tensor_scalar(negmax[:, half, :, 0, :], mx, -1.0, None, ALU.mult).then_inc(negmax_step, 1)
                wait_alone(pool, negmax_step, s.n(1, 4, 2 * half + 1), pool_passed)
                pool.tensor_tensor(maxdif[:, half, :, :], mx, negmax[:, half, :, 0, :], ALU.add).then_inc(negmax_step, 1)
                wait_alone(pool, negmax_step, s.n(1, 4, 2 * half + 2), pool_passed)
                pool.tensor_scalar(negmax[:, half, :, 1, :], maxdif[:, half, :, :], -1.0, None, ALU.mult).then_inc(negmax_ready, 1)

            def step(s):
                if s.has(2):
                    split(s)
                if s.has(1):
                    split_max(s, 0)
                if s.has(3):
                    tokens(s)
                if s.has(1):
                    split_max(s, 1)

            pipeline(pool, plan, step)


def attention64(nc, m, w):
    jobs = BATCHES * L0_PAIRS
    plan = Plan(jobs=jobs, weights=L0_PAIRS, unroll=L0_PAIRS, first=L0_PAIRS + 2,
                           rounds=BATCHES - 2, drain=2)
    with ExitStack() as ctx:
        sem, sb, begin = stage(nc, ctx, "a64")
        xcur = sb("xcur", [P, SEQ])
        qT = sb("qT", [P, 2, SEQ])
        kT = sb("kT", [P, 2, 2, SEQ])
        v = sb("v", [P, 2, 4, L0_HD])
        vr = sb("vr", [P, 2, 4, L0_HD])
        probs = sb("probs", [P, 2, 2, 384])
        negmax = sb("negmax", [P, 2, 4])
        sums = sb("sums", [P, 2, 4])
        rsum = sb("rsum", [P, 2, 4])
        zT = sb("zT", [P, 2, SEQ])
        pb = lambda n: ctx.enter_context(nc.psum_tensor(f"a64_{n}", [P, 512], F32))
        psQ, psV, psZ, psX = pb("psQ"), pb("psV"), pb("psZ"), pb("psX")
        psS = [[pb(f"psS{a}{h}") for h in range(2)] for a in range(2)]
        preset, tokens_ready = sem("preset"), sem("tokens_ready")
        qk_projected, q_ready, k_ready = sem("qk_projected"), sem("q_ready"), sem("k_ready")
        v_projected, v_ready, scores_ready, negmax_ready = sem("v_projected"), sem("v_ready"), sem("scores_ready"), sem("negmax_ready")
        exp_done, rsum_ready, vr_ready = sem("exp_done"), sem("rsum_ready"), sem("vr_ready")
        pv_ready, zT_ready, out_done, x_updated = sem("pv_ready"), sem("zT_ready"), sem("out_done"), sem("x_updated")
        out_step, pool_passed = sem("out_step"), sem("pool_passed")
        block = begin()

        @block.gpsimd
        def _(pool):
            pool.memset(kT[:, :, :, :], 0.0).then_inc(preset, 1)

            def step(s):
                if s.has(2) and (s.at + 2) % L0_PAIRS == 0:
                    if s.known(2, 1):
                        wait_alone(pool, v_projected, s.n(2), pool_passed)
                    pool.tensor_copy(xcur[:, :], m.xT16[:, s.batch(2), :]).then_inc(tokens_ready, 1)
                if s.has(-1):
                    wait_alone(pool, rsum_ready, s.n(-1, 1, 1), pool_passed)
                    if s.known(-1, 2):
                        wait_alone(pool, pv_ready, s.n(-1, 1, -1), pool_passed)
                    pool.tensor_tensor(vr[:, s.parity(-1), :, :], v[:, s.parity(-1), :, :],
                                       rsum[:, s.parity(-1), :].unsqueeze(2).to_broadcast([P, 4, L0_HD]), ALU.mult).then_inc(vr_ready, 1)

            pipeline(pool, plan, step)

        @block.tensor
        def _(pe):
            pe.wait_ge(preset, 1)

            def scores(s, h):
                a = s.parity(0)
                if h == 0:
                    pe.wait_ge(q_ready, s.n(0, 1, 1))
                    pe.wait_ge(k_ready, s.n(0, 1, 1))
                if s.known(0, 2):
                    pe.wait_ge(exp_done, s.n(0, 2, h - 3))
                ps = psS[a][h]
                pe.matmul(ps[:, 0:P], m.identity_bf[:, :], m.causal[:, :], start=True, stop=False, skip_group_check=True)
                pe.matmul(ps[:, 0:SEQ], kT[:, a, h, 0:P], qT[:, a, :], start=False, stop=True, skip_group_check=True)
                pe.matmul(ps[:, SEQ:384], kT[:, a, h, P:SEQ], qT[:, a, P:SEQ], start=True, stop=False, skip_group_check=True)
                pe.matmul(ps[:, SEQ:384], m.identity_bf[:, :], m.causal[:, :], start=False, stop=True, skip_group_check=True).then_inc(scores_ready, 1)

            def project(s):
                p = s.expert(1)
                if p == 0:
                    pe.wait_ge(tokens_ready, s.batch(1) + 1)
                if s.known(1, 1):
                    pe.wait_ge(q_ready, s.n(1))
                    pe.wait_ge(k_ready, s.n(1))
                pe.matmul(psQ[:, 0:SEQ], w.wq[:, p * P:(p + 1) * P], xcur[:, :], start=True, stop=True)
                pe.matmul(psQ[:, SEQ:512], w.wk[:, p * P:(p + 1) * P], xcur[:, :], start=True, stop=True).then_inc(qk_projected, 1)
                if s.known(1, 1):
                    pe.wait_ge(v_ready, s.n(1))
                for t in range(2):
                    mm = pe.matmul(psV[:, t * P:(t + 1) * P], xcur[:, t * P:(t + 1) * P], w.wv[:, p * P:(p + 1) * P], start=True, stop=True)
                mm.then_inc(v_projected, 1)

            def prob_values(s):
                b = s.parity(-1)
                pe.wait_ge(vr_ready, s.n(-1, 1, 1))
                if s.known(-1, 1):
                    pe.wait_ge(zT_ready, s.n(-1))
                for h in range(2):
                    pe.matmul(psZ[64 * h:64 * h + 64, P:SEQ], vr[:, b, 2 * h + 1, :], probs[:, b, h, SEQ:384], start=True, stop=False,
                              tile_position=(0, 64 * h), skip_group_check=True)
                for h in range(2):
                    mm = pe.matmul(psZ[64 * h:64 * h + 64, 0:SEQ], vr[:, b, 2 * h, :], probs[:, b, h, 0:SEQ], start=False, stop=True,
                                   tile_position=(0, 64 * h), skip_group_check=True)
                mm.then_inc(pv_ready, 1)

            def project_out(s):
                p, b = s.expert(-2), s.parity(-2)
                pe.wait_ge(zT_ready, s.n(-2, 1, 1))
                if p == 0 and s.at - 2 >= L0_PAIRS:
                    pe.wait_ge(x_updated, s.batch(-2))
                for t in range(2):
                    mm = pe.matmul(psX[:, t * D:(t + 1) * D], zT[:, b, t * P:(t + 1) * P], w.wo[:, p, :],
                                   start=(p == 0 and t == 0), stop=False, skip_group_check=True)
                mm.then_inc(out_step, 1)
                if p == L0_PAIRS - 1:
                    for t in range(2):
                        mm = pe.matmul(psX[:, t * D:(t + 1) * D], m.ones[:, :], w.bo[:, :], start=False, stop=True, skip_group_check=True)
                    mm.then_inc(out_done, 1)

            def step(s):
                if s.has(0):
                    scores(s, 0)
                if s.has(1):
                    project(s)
                if s.has(0):
                    scores(s, 1)
                if s.has(-2):
                    project_out(s)
                if s.has(-1):
                    prob_values(s)

            pipeline(pe, plan, step)

        @block.scalar
        def _(act):
            def step(s):
                if s.has(1):
                    act.wait_ge(qk_projected, s.n(1, 1, 1))
                    if s.known(1, 2):
                        act.wait_ge(scores_ready, s.n(1, 2, -2))
                    p = s.expert(1)
                    act.activation(qT[:, s.parity(1), :], psQ[:, 0:SEQ], ACT.Identity, bias=w.bqk[:, p, 0:1]).then_inc(q_ready, 1)
                if s.has(0):
                    a = s.parity(0)
                    for h in range(2):
                        act.wait_ge(negmax_ready, s.n(0, 2, h + 1))
                        if h == 0 and s.known(0, 2):
                            act.wait_ge(pv_ready, s.n(0, 1, -1))
                        act.activation(probs[:, a, h, 0:SEQ], psS[a][h][:, 0:SEQ], ACT.Exp, bias=negmax[:, a, 2 * h:2 * h + 1],
                                       accum_out=sums[:, a, 2 * h:2 * h + 1])
                        act.activation(probs[:, a, h, SEQ:384], psS[a][h][:, SEQ:384], ACT.Exp, bias=negmax[:, a, 2 * h + 1:2 * h + 2],
                                       accum_out=sums[:, a, 2 * h + 1:2 * h + 2]).then_inc(exp_done, 1)
                if s.has(-1):
                    act.wait_ge(pv_ready, s.n(-1, 1, 1))
                    if s.known(-1, 2):
                        act.wait_ge(out_step, s.n(-1, 1, -1))
                    act.activation(zT[:, s.parity(-1), :], psZ[:, 0:SEQ], ACT.Copy).then_inc(zT_ready, 1)

            pipeline(act, plan, step)

        @block.vector
        def _(dve):
            dve.wait_ge(preset, 1)

            def step(s):
                if s.has(0):
                    a = s.parity(0)
                    for h in range(2):
                        dve.wait_ge(scores_ready, s.n(0, 2, h + 1))
                        if s.known(0, 2):
                            dve.wait_ge(exp_done, s.n(0, 2, h - 3))
                        dve.tensor_reduce(negmax[:, a, 2 * h:2 * h + 1], psS[a][h][:, 0:SEQ], AX_X, ALU.max, negate=True)
                        dve.tensor_reduce(negmax[:, a, 2 * h + 1:2 * h + 2], psS[a][h][:, SEQ:384], AX_X, ALU.max,
                                          negate=True).then_inc(negmax_ready, 1)
                        if h == 0 and s.has(1):
                            take_kv(s)
                if s.has(1) and not s.has(0):
                    take_kv(s)
                if s.has(0):
                    dve.wait_ge(exp_done, s.n(0, 2, 2))
                    if s.known(0, 2):
                        dve.wait_ge(vr_ready, s.n(0, 1, -1))
                    dve.reciprocal(rsum[:, s.parity(0), :], sums[:, s.parity(0), :]).then_inc(rsum_ready, 1)
                if s.has(-2) and s.expert(-2) == L0_PAIRS - 1:
                    b = s.batch(-2)
                    dve.wait_ge(out_done, b + 1)
                    dve.tensor_tensor(m.x16[:, b, :], psX[:, 0:SEQ], m.x16[:, b, :], ALU.add).then_inc(x_updated, 1)

            def take_kv(s):
                c, p = s.parity(1), s.expert(1)
                dve.wait_ge(q_ready, s.n(1, 1, 1))
                for h in range(2):
                    r = slice(64 * h, 64 * h + 64)
                    k = dve.tensor_scalar(kT[r, c, h, :], psQ[r, SEQ:512], w.bqk[r, p, 1:2], None, ALU.add)
                k.then_inc(k_ready, 1)
                dve.wait_ge(v_projected, s.n(1, 1, 1))
                if s.known(1, 2):
                    dve.wait_ge(vr_ready, s.n(1, 1, -1))
                dve.tensor_tensor(v[:, c, :, :].rearrange("p (h t) d -> p t h d", h=2),
                                  psV[:, 0:SEQ].rearrange("p (t h d) -> p t h d", t=2, h=2),
                                  w.bv[:, p * P:(p + 1) * P].rearrange("p (h d) -> p h d", h=2).unsqueeze(1).to_broadcast([P, 2, 2, L0_HD]),
                                  ALU.add).then_inc(v_ready, 1)

            pipeline(dve, plan, step)


def swiglu(nc, m, name, w):
    with ExitStack() as ctx:
        sem, sb, begin = stage(nc, ctx, name)
        silu = sb("silu", [P, 2, 512])
        hidden = sb("hidden", [P, 2, HCH, 512])
        pb = lambda n: ctx.enter_context(nc.psum_tensor(f"{name}_{n}", [P, 512], F32))
        gate, up, out = [pb("gate0"), pb("gate1")], [pb("up0"), pb("up1")], [pb("out0"), pb("out1")]
        projected, silu_ready, hidden_ready, out_ready, x_updated = (
            sem("projected"), sem("silu_ready"), sem("hidden_ready"), sem("out_ready"), sem("x_updated"))
        block = begin()
        plan = Plan(jobs=GROUPS, weights=1, unroll=2, first=2, rounds=(GROUPS - 3) // 2, drain=1)

        def bank(s, c):
            return (s.at * HCH + c) % 2

        @block.tensor
        def _(pe):
            def step(s):
                for c in range(HCH):
                    if s.has(0):
                        if s.known(0, 1) or c >= 2:
                            pe.wait_ge(hidden_ready, s.n(0, HCH, c - 1))
                        b, g = bank(s, c), s.batch(0)
                        pe.matmul(gate[b][:, :], w.gate[:, c * P:(c + 1) * P], m.xT8[:, g, :], start=True, stop=True)
                        pe.matmul(up[b][:, :], w.up[:, c * P:(c + 1) * P], m.xT8[:, g, :], start=True, stop=True).then_inc(projected, 1)
                    if c == 0 and s.has(-1):
                        h = s.parity(-1)
                        pe.wait_ge(hidden_ready, s.n(-1, HCH, HCH))
                        if s.known(-1, 2):
                            pe.wait_ge(x_updated, s.n(-1, 1, -1))
                        for t in range(4):
                            for k in range(HCH):
                                mm = pe.matmul(out[h][:, t * D:(t + 1) * D], hidden[:, h, k, t * P:(t + 1) * P], w.down[:, k, :],
                                               start=(k == 0), stop=(k == HCH - 1))
                        mm.then_inc(out_ready, 1)

            pipeline(pe, plan, step)

        @block.scalar
        def _(act):
            def step(s):
                if s.has(0):
                    for c in range(HCH):
                        act.wait_ge(projected, s.n(0, HCH, c + 1))
                        if s.known(0, 1) or c >= 2:
                            act.wait_ge(hidden_ready, s.n(0, HCH, c - 1))
                        b = bank(s, c)
                        act.activation(silu[:, b, :], gate[b][:, :], ACT.Silu).then_inc(silu_ready, 1)

            pipeline(act, plan, step)

        @block.vector
        def _(dve):
            def step(s):
                for c in range(HCH):
                    if s.has(0):
                        b = bank(s, c)
                        dve.wait_ge(silu_ready, s.n(0, HCH, c + 1))
                        if c == 0 and s.known(0, 2):
                            dve.wait_ge(out_ready, s.n(0, 1, -1))
                        dve.tensor_tensor(hidden[:, s.parity(0), c, :], silu[:, b, :], up[b][:, :], ALU.mult).then_inc(hidden_ready, 1)
                    if c == 1 and s.has(-1):
                        g = s.batch(-1)
                        dve.wait_ge(out_ready, s.n(-1, 1, 1))
                        dve.tensor_tensor(m.xg[:, g, :], out[s.parity(-1)][:, :], m.xg[:, g, :], ALU.add).then_inc(x_updated, 1)

            pipeline(dve, plan, step)


def sign_mlp(nc, m, w):
    CH = FF3 // P
    with ExitStack() as ctx:
        sem, sb, begin = stage(nc, ctx, "mlp")
        h0 = sb("h0", [P, 2, CH, 512])
        h1 = sb("h1", [P, CH, 512])
        pb = lambda n: ctx.enter_context(nc.psum_tensor(f"mlp_{n}", [P, 512], F32))
        banks0, banks1, out = [pb("a0"), pb("a1")], [pb("b0"), pb("b1")], [pb("out0"), pb("out1")]
        p0, h0_ready, p1, h1_ready, out_ready, x_updated = (sem("p0"), sem("h0_ready"), sem("p1"), sem("h1_ready"), sem("out_ready"), sem("x_updated"))
        block = begin()
        plan = Plan(jobs=GROUPS, weights=1, unroll=2, first=2, rounds=(GROUPS - 4) // 2, drain=1)

        @block.tensor
        def _(pe):
            def step(s):
                for c in range(CH):
                    if s.has(1):
                        if s.known(1, 1) or c >= 2:
                            pe.wait_ge(h0_ready, s.n(1, CH, c - 1))
                        pe.matmul(banks0[c % 2][:, :], w.k0[:, c * P:(c + 1) * P], m.xT8[:, s.batch(1), :], start=True, stop=True).then_inc(p0, 1)
                    if c == 1 and s.has(-1):
                        pe.wait_ge(h1_ready, s.n(-1, CH, CH))
                        if s.known(-1, 2):
                            pe.wait_ge(x_updated, s.n(-1, 1, -1))
                        for t in range(4):
                            for k in range(CH):
                                mm = pe.matmul(out[s.parity(-1)][:, t * D:(t + 1) * D], h1[:, k, t * P:(t + 1) * P], w.k2[:, k, :],
                                               start=(k == 0), stop=(k == CH - 1))
                        mm.then_inc(out_ready, 1)
                    if s.has(0):
                        if c == 0:
                            pe.wait_ge(h0_ready, s.n(0, CH, CH))
                        if s.known(0, 1) or c >= 2:
                            pe.wait_ge(h1_ready, s.n(0, CH, c - 1))
                        for k in range(CH):
                            mm = pe.matmul(banks1[c % 2][:, :], w.k1[:, k, c * P:(c + 1) * P], h0[:, s.parity(0), k, :],
                                           start=(k == 0), stop=(k == CH - 1))
                        mm.then_inc(p1, 1)

            pipeline(pe, plan, step)

        @block.scalar
        def _(act):
            def step(s):
                for c in range(CH):
                    if s.has(1):
                        act.wait_ge(p0, s.n(1, CH, c + 1))
                        if c == 0 and s.known(1, 2):
                            act.wait_ge(p1, s.n(1, CH, -CH))
                        act.activation(h0[:, s.parity(1), c, :], banks0[c % 2][:, :], ACT.Relu, scale=w.s[:, 0:1]).then_inc(h0_ready, 1)

            pipeline(act, plan, step)

        @block.vector
        def _(dve):
            def step(s):
                for c in range(CH):
                    if c == 2 and s.has(-1):
                        g = s.batch(-1)
                        dve.wait_ge(out_ready, s.n(-1, 1, 1))
                        dve.scalar_tensor_tensor(out=m.xg[:, g, :], in0=out[s.parity(-1)][:, :], scalar=w.s[:, 2:3], in1=m.xg[:, g, :],
                                                 op0=ALU.mult, op1=ALU.add).then_inc(x_updated, 1)
                    if s.has(0):
                        dve.wait_ge(p1, s.n(0, CH, c + 1))
                        if c == 0 and s.known(0, 1):
                            dve.wait_ge(out_ready, s.n(0))
                        dve.tensor_scalar(h1[:, c, :], banks1[c % 2][:, :], w.s[:, 1:2], 0.0, ALU.mult, ALU.max).then_inc(h1_ready, 1)

            pipeline(dve, plan, step)


def fourier_attention(nc, m, w):
    F2 = 2 * FREQS
    with ExitStack() as ctx:
        sem, sb, begin = stage(nc, ctx, "fft")
        xcur = sb("xcur", [P, 2, SEQ])
        kqv = sb("kqv", [P, 2, 2, 3 * F2])
        square = sb("square", [P, 2, 2 * F2])
        power = sb("power", [P, 2, 2, FREQS])
        size = sb("size", [P, 2, 2, FREQS])
        inverse = sb("inverse", [P, 2, 2, FREQS])
        prod = sb("prod", [P, 2, F2])
        cross = sb("cross", [P, 2, 2, FREQS])
        kv = sb("kv", [P, 2, 2, F2])
        qT = sb("qT", [FREQS, 2, SEQ])
        total = sb("total", [FREQS, 2, SEQ])
        straight = sb("straight", [FREQS, 2, SEQ])
        across = sb("across", [FREQS, 2, SEQ])
        final = sb("final", [FREQS, 2, SEQ])
        pb = lambda n: ctx.enter_context(nc.psum_tensor(f"fft_{n}", [P, 512], F32))
        psP, psQ, psC, psX = [pb("psP0"), pb("psP1")], pb("psQ"), pb("psC"), pb("psX")
        tokens_ready, projected, kqv_ready, dve_step, power_ready, size_ready = (
            sem("tokens_ready"), sem("projected"), sem("kqv_ready"), sem("dve_step"), sem("power_ready"), sem("size_ready"))
        unit_ready, kv_ready, q_turned, qT_ready, total_ready, total_copied, final_ready, out_ready, x_updated = (
            sem("unit_ready"), sem("kv_ready"), sem("q_turned"), sem("qT_ready"), sem("total_ready"), sem("total_copied"),
            sem("final_ready"), sem("out_ready"), sem("x_updated"))
        pool_passed, across_ready = sem("pool_passed"), sem("across_ready")
        block = begin()
        plan = Plan(jobs=BATCHES, weights=1, unroll=2, first=2, rounds=(BATCHES - 4) // 2, drain=0)
        K, Q, V = (slice(i * F2, (i + 1) * F2) for i in range(3))

        def halves(a):
            return a.rearrange("p t (c f) -> p t c f", c=2)

        @block.gpsimd
        def _(pool):
            def step(s):
                if s.has(2):
                    if s.known(2, 2):
                        wait_alone(pool, projected, s.n(0, 1, 1), pool_passed)
                    pool.tensor_copy(xcur[:, s.parity(2), :], m.xT16[:, s.batch(2), :]).then_inc(tokens_ready, 1)

            pipeline(pool, plan, step)

        @block.tensor
        def _(pe):
            def step(s):
                if s.has(1):
                    c = s.parity(1)
                    pe.wait_ge(tokens_ready, s.n(1, 1, 1))
                    if s.known(1, 1):
                        pe.wait_ge(kqv_ready, s.n(1))
                    for t in range(2):
                        mm = pe.matmul(psP[t][:, 0:3 * F2], xcur[:, c, t * P:(t + 1) * P], w.kqv[:, :], start=True, stop=True)
                    mm.then_inc(projected, 1)
                if s.has(0):
                    a = s.parity(0)
                    pe.wait_ge(kv_ready, s.n(0, 1, 1))
                    if s.known(0, 1):
                        pe.wait_ge(total_copied, s.n(0))
                    for i in range(2):
                        f = slice(i * FREQS, (i + 1) * FREQS)
                        o = psC[0:FREQS, i * SEQ:(i + 1) * SEQ]
                        pe.matmul(o, kv[:, a, 0, f], m.upto[:, :], start=True, stop=False, skip_group_check=True)
                        mm = pe.matmul(o[:, P:SEQ], kv[:, a, 1, f], m.upto[:, 0:P], start=False, stop=True, skip_group_check=True)
                    mm.then_inc(total_ready, 1)
                    pe.wait_ge(final_ready, s.n(0, 1, 1))
                    if s.known(0, 1):
                        pe.wait_ge(x_updated, s.n(0))
                    for t in range(2):
                        for i in range(2):
                            mm = pe.matmul(psX[:, t * D:(t + 1) * D], final[:, i, t * P:(t + 1) * P], w.back[:, i, :], start=(i == 0), stop=(i == 1))
                    mm.then_inc(out_ready, 1)
                if s.has(1):
                    c = s.parity(1)
                    pe.wait_ge(unit_ready, s.n(1, 1, 1))
                    if s.known(1, 1):
                        pe.wait_ge(qT_ready, s.n(1))
                    for i in range(2):
                        for t in range(2):
                            mm = pe.transpose(psQ[0:FREQS, i * SEQ + t * P:i * SEQ + (t + 1) * P],
                                              kqv[:, c, t, F2 + i * FREQS:F2 + (i + 1) * FREQS], m.identity[:, :])
                    mm.then_inc(q_turned, 1)

            pipeline(pe, plan, step)

        @block.scalar
        def _(act):
            def step(s):
                if s.has(1):
                    c = s.parity(1)
                    act.wait_ge(projected, s.n(1, 1, 1))
                    if s.known(1, 2):
                        act.wait_ge(q_turned, s.n(1, 1, -1))
                    for t in range(2):
                        k = act.activation(kqv[:, c, t, :], psP[t][:, 0:3 * F2], ACT.Copy)
                    k.then_inc(kqv_ready, 1)
                if s.has(0):
                    act.wait_ge(total_ready, s.n(0, 1, 1))
                    if s.known(0, 1):
                        act.wait_ge(final_ready, s.n(0))
                    act.activation(total[:, :, :], psC[0:FREQS, :], ACT.Copy).then_inc(total_copied, 1)
                if s.has(1):
                    act.wait_ge(power_ready, s.n(1, 1, 1))
                    act.activation(size[:, :, :, :], power[:, :, :, :], ACT.Sqrt).then_inc(size_ready, 1)
                    act.wait_ge(q_turned, s.n(1, 1, 1))
                    if s.known(1, 1):
                        act.wait_ge(final_ready, s.n(1))
                    act.activation(qT[:, :, :], psQ[0:FREQS, :], ACT.Copy).then_inc(qT_ready, 1)

            pipeline(act, plan, step)

        @block.vector
        def _(dve):
            def step(s):
                if s.has(1):
                    c = s.parity(1)
                    kq = kqv[:, c, :, 0:2 * F2]
                    dve.wait_ge(kqv_ready, s.n(1, 1, 1))
                    dve.tensor_tensor(square[:, :, :], kq, kq, ALU.mult).then_inc(dve_step, 1)
                    dve.wait_ge(dve_step, s.n(1, 8, 1))
                    sq = square[:, :, :].rearrange("p t (c i f) -> p t c i f", c=2, i=2)
                    dve.tensor_tensor(power[:, :, :, :], sq[:, :, :, 0, :], sq[:, :, :, 1, :], ALU.add).then_inc(power_ready, 1)
                if s.has(0):
                    dve.wait_ge(total_copied, s.n(0, 1, 1))
                    dve.wait_ge(qT_ready, s.n(0, 1, 1))
                    dve.tensor_tensor(straight[:, :, :], total[:, :, :], qT[:, :, :], ALU.mult).then_inc(across_ready, 1)
                    dve.tensor_tensor(across[:, 0, :], total[:, 1, :], qT[:, 0, :], ALU.mult).then_inc(across_ready, 1)
                    dve.tensor_tensor(across[:, 1, :], total[:, 0, :], qT[:, 1, :], ALU.mult).then_inc(across_ready, 1)
                    dve.wait_ge(across_ready, s.n(0, 3, 3))
                    if s.known(0, 1):
                        dve.wait_ge(out_ready, s.n(0))
                    dve.tensor_tensor(final[:, 0, :], straight[:, 0, :], straight[:, 1, :], ALU.add)
                    dve.tensor_tensor(final[:, 1, :], across[:, 0, :], across[:, 1, :], ALU.subtract).then_inc(final_ready, 1)
                if s.has(1):
                    c = s.parity(1)
                    dve.wait_ge(size_ready, s.n(1, 1, 1))
                    dve.tensor_scalar(size[:, :, :, :], size[:, :, :, :], 1e-8, None, ALU.add).then_inc(dve_step, 1)
                    dve.wait_ge(dve_step, s.n(1, 8, 2))
                    dve.reciprocal(inverse[:, :, :, :], size[:, :, :, :]).then_inc(dve_step, 1)
                    dve.wait_ge(dve_step, s.n(1, 8, 3))
                    for i, part in enumerate((K, Q)):
                        a = halves(kqv[:, c, :, part])
                        u = dve.tensor_tensor(a, a, inverse[:, :, i, :].unsqueeze(2).to_broadcast([P, 2, 2, FREQS]), ALU.mult)
                        u.then_inc(unit_ready if i else dve_step, 1)
                    dve.wait_ge(dve_step, s.n(1, 8, 4))
                    k, v = kqv[:, c, :, K], kqv[:, c, :, V]
                    k2, v2 = halves(k), halves(v)
                    dve.tensor_tensor(prod[:, :, :], k, v, ALU.mult).then_inc(dve_step, 1)
                    dve.tensor_tensor(cross[:, :, 0, :], k2[:, :, 0, :], v2[:, :, 1, :], ALU.mult).then_inc(dve_step, 1)
                    dve.tensor_tensor(cross[:, :, 1, :], k2[:, :, 1, :], v2[:, :, 0, :], ALU.mult).then_inc(dve_step, 1)
                    dve.wait_ge(dve_step, s.n(1, 8, 7))
                    if s.known(1, 2):
                        dve.wait_ge(total_ready, s.n(1, 1, -1))
                    p2 = halves(prod[:, :, :])
                    dve.tensor_tensor(kv[:, c, :, 0:FREQS], p2[:, :, 0, :], p2[:, :, 1, :], ALU.subtract).then_inc(dve_step, 1)
                    dve.tensor_tensor(kv[:, c, :, FREQS:F2], cross[:, :, 0, :], cross[:, :, 1, :], ALU.add).then_inc(kv_ready, 1)
                if s.has(0):
                    dve.wait_ge(out_ready, s.n(0, 1, 1))
                    b = s.batch(0)
                    dve.tensor_tensor(m.x16[:, b, :], psX[:, 0:SEQ], m.x16[:, b, :], ALU.add).then_inc(x_updated, 1)

            pipeline(dve, plan, step)


def router(nc, m, w):
    with ExitStack() as ctx:
        sem, sb, begin = stage(nc, ctx, "router")
        logitsT = sb("logitsT", [EXPERTS, TILES * P])
        lg = sb("lg", [P, TILES, EXPERTS])
        prob = sb("prob", [P, TILES, EXPERTS])
        rank = sb("rank", [P, TILES, EXPERTS])
        member = sb("member", [P, TILES, EXPERTS])
        compare = sb("compare", [P, 12, TILES])
        col = sb("col", [P, 3, TILES])
        anyone = sb("anyone", [P, BATCHES, 2, EXPERTS])
        counts = sb("counts", [P, BATCHES, 2, EXPERTS])
        mask = sb("mask", [P, 2, BATCHES, EXPERTS])
        maskT = sb("maskT", [P, P], BF16)
        psL = [ctx.enter_context(nc.psum_tensor(f"router_psL{k}", [P, 512], F32)) for k in range(2)]
        psT = ctx.enter_context(nc.psum_tensor("router_psT", [P, 512], F32))
        logits_ready, logitsT_ready, turned, step_done, top_ready, exp_ready, member_ready, counted, mask_ready, mask_turned, maskT_ready, saved = (
            sem(n) for n in ("logits_ready", "logitsT_ready", "turned", "step_done", "top_ready", "exp_ready", "member_ready",
                             "counted", "mask_ready", "mask_turned", "maskT_ready", "saved"))
        block = begin()

        @block.tensor
        def _(pe):
            for g in range(GROUPS):
                if g >= 2:
                    pe.wait_ge(logitsT_ready, g - 1)
                pe.matmul(psL[g % 2][0:EXPERTS, :], w.router[:, :], m.xT8[:, g, :], start=True, stop=True).then_inc(logits_ready, 1)
            pe.wait_ge(logitsT_ready, GROUPS)
            for t in range(TILES):
                mm = pe.transpose(psT[:, EXPERTS * t:EXPERTS * (t + 1)], logitsT[:, t * P:(t + 1) * P], m.identity[0:EXPERTS, 0:EXPERTS])
            mm.then_inc(turned, 1)
            pe.wait_ge(member_ready, 1)
            pe.matmul(psL[0][:, 0:P], m.ones[:, :], member[:, :, :].rearrange("p t e -> p (t e)"), start=True, stop=True).then_inc(counted, 1)
            pe.wait_ge(mask_ready, 1)
            pe.transpose(psL[1][:, 0:P], mask[:, :, :, :].rearrange("p t b e -> p (t b e)"), m.identity[:, :]).then_inc(mask_turned, 1)

        @block.scalar
        def _(act):
            for g in range(GROUPS):
                act.wait_ge(logits_ready, g + 1)
                act.activation(logitsT[:, g * 512:(g + 1) * 512], psL[g % 2][0:EXPERTS, :], ACT.Identity, bias=w.router_b[:, 0:1]).then_inc(logitsT_ready, 1)
            act.wait_ge(top_ready, 1)
            act.activation(prob[:, :, :], lg[:, :, :], ACT.Exp).then_inc(exp_ready, 1)
            act.wait_ge(mask_turned, 1)
            act.activation(maskT[:, :], psL[1][:, 0:P], ACT.Copy).then_inc(maskT_ready, 1)

        @block.sync
        def _(sp):
            sp.wait_ge(maskT_ready, 1)
            for t in range(2):
                rows = slice(t * BATCHES * EXPERTS, (t + 1) * BATCHES * EXPERTS)
                sp.dma_start(m.mask_dram.rearrange("b e k -> (b e) k")[:, t * P:(t + 1) * P], maskT[rows, :]).then_inc(saved, 16)
            sp.wait_ge(saved, 32)

        @block.vector
        def _(dve):
            n = [0]

            def chain(ins):
                n[0] += 1
                ins.then_inc(step_done, 1)
                dve.wait_ge(step_done, n[0])

            dve.wait_ge(turned, 1)
            logits = psT[:, 0:TILES * EXPERTS].rearrange("p (t e) -> p t e", e=EXPERTS)
            over_e = lambda a: a.unsqueeze(2).to_broadcast([P, TILES, EXPERTS])
            chain(dve.tensor_reduce(col[:, 0, :], logits, AX_X, ALU.max))
            dve.tensor_tensor(lg[:, :, :], logits, over_e(col[:, 0, :]), ALU.subtract).then_inc(top_ready, 1)
            dve.wait_ge(exp_ready, 1)
            chain(dve.tensor_reduce(col[:, 1, :], prob[:, :, :], AX_X, ALU.add))
            chain(dve.reciprocal(col[:, 2, :], col[:, 1, :]))
            chain(dve.tensor_tensor(prob[:, :, :], prob[:, :, :], over_e(col[:, 2, :]), ALU.mult))
            k = 0
            for e in range(EXPERTS):
                for o in range(EXPERTS):
                    if o != e:
                        last = dve.tensor_tensor(compare[:, k, :], prob[:, :, o], prob[:, :, e], ALU.is_ge if o < e else ALU.is_gt)
                        k += 1
            chain(last)
            for e in range(EXPERTS):
                last = dve.tensor_tensor(rank[:, :, e], compare[:, 3 * e, :], compare[:, 3 * e + 1, :], ALU.add)
            chain(last)
            for e in range(EXPERTS):
                last = dve.tensor_tensor(rank[:, :, e], rank[:, :, e], compare[:, 3 * e + 2, :], ALU.add)
            chain(last)
            dve.tensor_scalar(member[:, :, :], rank[:, :, :], 2.0, None, ALU.is_lt).then_inc(member_ready, 1)
            dve.wait_ge(member_ready, 1)
            dve.tensor_tensor(m.gate[:, :, :, :].rearrange("p b t e -> p (b t) e"), prob[:, :, :], member[:, :, :], ALU.mult)
            dve.wait_ge(counted, 1)
            chain(dve.tensor_copy(counts[:, :, :, :].rearrange("p b t e -> p (b t e)"), psL[0][:, 0:P]))
            for t in range(2):
                last = dve.tensor_tensor(anyone[:, :, t, :], counts[:, :, 0, :], counts[:, :, 1, :], ALU.add)
            chain(last)
            chain(dve.tensor_scalar(anyone[:, :, :, :].rearrange("p b t e -> p (b t e)"), anyone[:, :, :, :].rearrange("p b t e -> p (b t e)"), 1.0, NEG, ALU.min, ALU.mult))
            chain(dve.tensor_scalar(member[:, :, :], member[:, :, :], -1.0, 1.0, ALU.mult, ALU.add))
            dve.tensor_tensor(mask[:, :, :, :].rearrange("p t b e -> p b t e"), member[:, :, :].rearrange("p (b t) e -> p b t e", t=2),
                              anyone[:, :, :, :], ALU.mult).then_inc(mask_ready, 1)


def load(nc, m, a):
    W = Weights
    ctx = m.ctx
    sb = lambda n, s, dt=F32: ctx.enter_context(nc.sbuf_tensor(n, s, dt))
    x = sb("x", [P, TILES, D])
    m.x4 = x[:, :, :].rearrange("p (g k) d -> p g k d", k=4)
    m.xg = x[:, :, :].rearrange("p (g k) d -> p g (k d)", k=4)
    m.x16 = x[:, :, :].rearrange("p (b t) d -> p b (t d)", t=2)
    m.x32 = x[:, :, :].rearrange("p (b t) d -> p b t d", t=2)
    xT = sb("xT", [P, TILES * P])
    m.xT8 = xT[:, :].rearrange("p (g n) -> p g n", n=512)
    m.xT16 = xT[:, :].rearrange("p (b n) -> p b n", n=SEQ)
    m.identity, m.identity_bf, m.ones = sb("identity", [P, P]), sb("identity_bf", [P, P], BF16), sb("ones", [P, P])
    m.causal, m.upto = sb("causal", [P, P], BF16), sb("upto", [P, SEQ])
    m.gate = sb("gate", [P, BATCHES, 2, EXPERTS])
    m.mask_dram = nc.dram_tensor("mask_dram", (BATCHES, EXPERTS, SEQ), BF16, kind="Internal").ap()

    loads = [(x[:, :, :], a["x"].rearrange("(t p) d -> p t d", p=P))]

    def held(name, shape, src, dt=F32):
        t = sb(name, shape, dt)
        full = t[tuple(slice(None) for _ in shape)]
        loads.append((full, src))
        return t

    def row_matrix(name, shape, src):
        t = sb(name, shape)
        rows.append(t)
        row_loads.append((t[0:1, :, :] if len(shape) == 3 else t[0:1, :], src))
        return t

    rows, row_loads = [], []
    bcast = lambda ap, n: ap.unsqueeze(0).to_broadcast([P, n])
    l0 = W(wq=held("l0_wq", [P, 1024], a["l0_w"][:, 0]), wk=held("l0_wk", [P, 1024], a["l0_w"][:, 1]), wv=held("l0_wv", [P, 1024], a["l0_w"][:, 2]),
           bqk=held("l0_bqk", [P, L0_PAIRS, 3], a["l0_bqk"]), bv=held("l0_bv", [P, 1024], bcast(a["l0_bv"], 1024)),
           wo=held("l0_wo", [P, L0_PAIRS, D], a["l0_wo"]), bo=row_matrix("l0_bo", [P, D], a["l0_bo"].unsqueeze(0)))
    ffn, ints = [], []
    for i in range(2):
        f = W(gate=sb(f"f{i}_gate", [P, HIDDEN]), up=sb(f"f{i}_up", [P, HIDDEN]), down=sb(f"f{i}_down", [P, HCH, D]))
        for n, t, shape in (("gate", f.gate, [P, HIDDEN]), ("up", f.up, [P, HIDDEN]), ("down", f.down, [P, HCH, D])):
            loads.append((t[:, :].bitcast(I32) if len(shape) == 2 else t[:, :, :].bitcast(I32), a[f"f{i}_{n}"]))
            ints.append(t[:, :] if len(shape) == 2 else t[:, :, :])
        ffn.append(f)

    def heads8(name, weights):
        return dict(wq=held(f"{name}_wq", [P, weights, D], a[f"{name}_wq"]), wk=held(f"{name}_wk", [P, weights, D], a[f"{name}_wk"]),
                    wv=held(f"{name}_wv", [P, weights, D], a[f"{name}_wv"]), wo=held(f"{name}_wo", [P, weights, D], a[f"{name}_wo"]),
                    bv=held(f"{name}_bv", [P, weights, D], a[f"{name}_bv"].unsqueeze(0).to_broadcast([P, weights, D])),
                    bo=row_matrix(f"{name}_bo", [P, weights, D], a[f"{name}_bo"].unsqueeze(0)))

    l1 = W(**heads8("l1", 1), bq=held("l1_bq", [P, 1], a["l1_bq"]), bk=held("l1_bk", [P, 1], a["l1_bk"]), qscale=1.0, ones_value=float(np.sqrt(np.float32(D))))
    l2 = W(**heads8("l2", EXPERTS), bq=held("l2_bq", [P, EXPERTS], a["l2_bq"]), bk=held("l2_bk", [P, EXPERTS], a["l2_bk"]), qscale=0.5, ones_value=1.0,
           router=held("l2_router", [P, EXPERTS], a["router_w"]), router_b=held("l2_router_b", [EXPERTS, 1], a["router_b"].unsqueeze(1)))
    l3 = W(**heads8("l3", 1), wq2=held("l3_wq2", [P, 1, D], a["l3_wq2"]), wk2=held("l3_wk2", [P, 1, D], a["l3_wk2"]),
           rot_bias=held("l3_rb", [P, 4], a["l3_rb"]), tables=held("l3_tables", [P, 2, 2, SEQ], a["c_rotary"]), ones_value=1.0)
    fold_in = held("fold_in", [P, 3, D], a["l2a_w"])
    dft = held("dft", [P, 2 * FREQS], a["c_dft"])
    fa = W(kqv=sb("fa_kqv", [P, 3 * 2 * FREQS]), back=held("fa_back", [FREQS, 2, D], a["c_idft"]))
    ku = [held("k0_bytes", [P, 2, FF3 // 4], a["k0"], I32)[:, :, :].bitcast(U8), held("k1_bytes", [P, 4, FF3 // 4], a["k1"], I32)[:, :, :].bitcast(U8),
          held("k2_bytes", [P, 4, D // 4], a["k2"], I32)[:, :, :].bitcast(U8)]
    mlp = W(k0=sb("k0", [P, FF3]), k1=sb("k1", [P, 4, FF3]), k2=sb("k2", [P, 4, D]), s=sb("s", [P, 3]))
    s_in = held("s_in", [P, 3], bcast(a["s"], 3))

    with ExitStack() as inner:
        sem, _, begin = stage(nc, inner, "load")
        loaded, zeroed, rows_loaded, pool_step, made, folded = (sem(n) for n in ("loaded", "zeroed", "rows_loaded", "pool_step", "made", "folded"))
        psF = inner.enter_context(nc.psum_tensor("load_psF", [P, 512], F32))
        block = begin()

        @block.sync
        def _(sp):
            for dst, src in loads:
                sp.dma_start(dst, src).then_inc(loaded, 16)
            sp.wait_ge(zeroed, len(rows))
            for dst, src in row_loads:
                sp.dma_start(dst, src).then_inc(rows_loaded, 16)
            sp.wait_ge(loaded, 16 * len(loads))
            sp.wait_ge(rows_loaded, 16 * len(rows))

        @block.gpsimd
        def _(pool):
            for t in rows:
                pool.memset(t[:, :, :] if len(t.shape) == 3 else t[:, :], 0.0).then_inc(zeroed, 1)
            pool.memset(m.identity[:, :], 0.0)
            pool.memset(m.ones[:, :], 1.0)
            pool.memset(m.causal[:, :], 0.0)
            pool.memset(m.upto[:, :], 1.0).then_inc(pool_step, 1)
            pool.wait_ge(pool_step, 1)
            pool.affine_select(out=m.identity[:, :], in_=m.identity[:, :], compare_op=ALU.not_equal, fill=1.0, base=0,
                               pattern=[[-1, P]], channel_multiplier=1).then_inc(pool_step, 1)
            pool.affine_select(out=m.causal[:, :], in_=m.causal[:, :], compare_op=ALU.is_ge, fill=NEG, base=0,
                               pattern=[[1, P]], channel_multiplier=-1)
            pool.affine_select(out=m.upto[:, 0:P], in_=m.upto[:, 0:P], compare_op=ALU.is_ge, fill=0.0, base=0,
                               pattern=[[1, P]], channel_multiplier=-1).then_inc(pool_step, 1)
            pool.wait_ge(pool_step, 2)
            pool.tensor_copy(m.identity_bf[:, :], m.identity[:, :]).then_inc(pool_step, 1)

        @block.tensor
        def _(pe):
            pe.wait_ge(loaded, 16 * len(loads))
            for i in range(3):
                mm = pe.matmul(psF[:, i * 2 * FREQS:(i + 1) * 2 * FREQS], fold_in[:, i, :], dft[:, :], start=True, stop=True)
            mm.then_inc(folded, 1)

        @block.vector
        def _(dve):
            dve.wait_ge(loaded, 16 * len(loads))
            for t in ints:
                dve.tensor_scalar(t, t.bitcast(I32), float(np.float32(1.0 / 127.0)), None, ALU.mult)
            dve.tensor_scalar(l2.bq[:, :], l2.bq[:, :], 0.5, None, ALU.mult)
            dve.tensor_scalar(mlp.s[:, 0:2], s_in[:, 0:2], 2.0, None, ALU.mult)
            dve.tensor_copy(mlp.s[:, 2:3], s_in[:, 2:3])
            dve.tensor_tensor(mlp.k0[:, :], ku[0][:, 0, :], ku[0][:, 1, :], ALU.subtract).then_inc(made, 1)
            dve.tensor_scalar(mlp.k1[:, :, :], ku[1][:, :, :], 2.0, -1.0, ALU.mult, ALU.add)
            dve.tensor_scalar(mlp.k2[:, :, :], ku[2][:, :, :], 2.0, -1.0, ALU.mult, ALU.add)
            dve.wait_ge(made, 1)
            dve.tensor_scalar(mlp.k0[:, :], mlp.k0[:, :], 2.0, None, ALU.mult)
            dve.wait_ge(folded, 1)
            dve.tensor_copy(fa.kqv[:, :], psF[:, 0:6 * FREQS])

    m.l0, m.ffn, m.l1, m.l2, m.l3, m.fa, m.mlp = l0, ffn, l1, l2, l3, fa, mlp


def network(nc, a, out, stop=99):
    m = Model(ExitStack())
    with m.ctx:
        load(nc, m, a)
        layers = [
            lambda: (layer_norm(nc, m, "n0", rms=True), attention64(nc, m, m.l0)),
            lambda: (layer_norm(nc, m, "n1"), swiglu(nc, m, "f0", m.ffn[0])),
            lambda: (layer_norm(nc, m, "n2"), attention8(nc, m, "a1", m.l1)),
            lambda: (layer_norm(nc, m, "n3"), swiglu(nc, m, "f1", m.ffn[1])),
            lambda: (layer_norm(nc, m, "n4", add_to_x=True), fourier_attention(nc, m, m.fa)),
            lambda: (layer_norm(nc, m, "n5"), router(nc, m, m.l2), attention8(nc, m, "a2", m.l2, weights=EXPERTS, masked=True)),
            lambda: (layer_norm(nc, m, "n6"), attention8(nc, m, "a3", m.l3, rotary=True)),
            lambda: (layer_norm(nc, m, "n7"), sign_mlp(nc, m, m.mlp)),
        ]
        for i, layer in enumerate(layers):
            if i in stop if isinstance(stop, tuple) else i < stop:
                layer()
        with nc.semaphore("stored") as stored, nc.Block() as block:
            @block.sync
            def _(sp):
                sp.dma_start(out.rearrange("(b t p) d -> p b t d", t=2, p=P), m.x32).then_inc(stored, 16)
                sp.wait_ge(stored, 16)


def constants():
    n, f = np.arange(D), np.arange(FREQS)
    angle = 2 * np.pi * ((n[:, None] * f[None, :]) % D) / D
    dft = np.concatenate([np.cos(angle), -np.sin(angle)], axis=1)
    dft[:, FREQS] = 0.0
    dft[:, 2 * FREQS - 1] = 0.0
    weight = np.where((f == 0) | (f == FREQS - 1), 1.0, 2.0)[:, None] / D
    idft = np.stack([weight * np.cos(angle.T), -weight * np.sin(angle.T)], axis=1)
    idft[0, 1, :] = 0.0
    idft[FREQS - 1, 1, :] = 0.0
    freqs = 10000.0 ** (np.arange(0, HD, 2) / HD)
    turn = (np.arange(SEQ)[None, :] * np.round(freqs)[:, None])
    cos, sin = np.cos(turn), np.sin(turn)
    rot = np.stack([np.concatenate([cos, cos]), np.concatenate([-sin, sin])])
    scale = np.array([np.float32(HD ** -0.5), 1.0])
    tables = np.repeat(rot[:, :, None, None, :] * scale[None, None, None, :, None], HEADS, axis=2)
    tables = tables.transpose(1, 2, 0, 3, 4).reshape(P, 2, 2, SEQ)
    return dft.astype(np.float32), idft.astype(np.float32), tables.astype(np.float32)


def lay_out(i):
    a = {k: np.asarray(v) for k, v in i.items()}
    c = np.ascontiguousarray
    o = {"x": a["L0_attn_x"].reshape(-1, D)}
    o["l0_w"] = a["L0_attn_W_qkv"].reshape(L0_HEADS, L0_HD, 3, D).transpose(3, 2, 0, 1).reshape(D, 3, 1024)
    b = a["L0_attn_b_qkv"].reshape(L0_PAIRS, 2, L0_HD, 3)
    o["l0_bqk"] = b.transpose(1, 2, 0, 3).reshape(P, L0_PAIRS, 3)
    o["l0_bv"] = b[:, :, :, 2].reshape(1024)
    o["l0_wo"] = a["L0_attn_W_o"].T.reshape(L0_PAIRS, P, D).transpose(1, 0, 2)
    o["l0_bo"] = a["L0_attn_b_o"]
    for n in range(2):
        o[f"f{n}_gate"] = a[f"L{n}_ffn_w_gate"].T
        o[f"f{n}_up"] = a[f"L{n}_ffn_w_up"].T
        o[f"f{n}_down"] = a[f"L{n}_ffn_w_down"].T.reshape(HCH, P, D).transpose(1, 0, 2)
    dh = lambda w: w.reshape(w.shape[:-1] + (HEADS, HD)).swapaxes(-1, -2).reshape(w.shape)

    w, b = a["L1_attn_W_qkv"], a["L1_attn_b_qkv"]
    o["l1_wq"], o["l1_wk"], o["l1_wv"], o["l1_wo"] = dh(w[:, 0:D])[:, None], dh(w[:, D:2 * D])[:, None], w[:, None, 2 * D:], a["L1_attn_W_out"][:, None]
    o["l1_bq"], o["l1_bk"], o["l1_bv"], o["l1_bo"] = dh(b[0:D])[:, None], dh(b[D:2 * D])[:, None], b[None, 2 * D:], a["L1_attn_b_out"][None]
    for n in "qkvo":
        w = a[f"L2_ffn_w{n}"].transpose(1, 0, 2)
        o[f"l2_w{n}"] = dh(w) if n in "qk" else w
    o["l2_bq"], o["l2_bk"] = dh(a["L2_ffn_bq"]).T, dh(a["L2_ffn_bk"]).T
    o["l2_bv"], o["l2_bo"] = a["L2_ffn_bv"], a["L2_ffn_bo"]
    o["router_w"], o["router_b"] = a["L2_ffn_router_w"], a["L2_ffn_router_b"]
    o["l2a_w"] = np.stack([a["L2_attn_Wk"], a["L2_attn_Wq"], a["L2_attn_Wv"]], axis=1)

    def rotated(w, partner):
        v = w.reshape(w.shape[:-1] + (HEADS, HD // 2, 2))
        v = np.moveaxis(v, (-1, -2, -3), (-3, -2, -1))
        if partner:
            v = v[..., ::-1, :, :]
        return v.reshape(w.shape)

    w, b = a["L3_attn_qkv_w"], a["L3_attn_qkv_b"]
    for n, at in (("q", 0), ("k", D)):
        o[f"l3_w{n}"], o[f"l3_w{n}2"] = rotated(w[:, at:at + D], False)[:, None], rotated(w[:, at:at + D], True)[:, None]
    o["l3_rb"] = np.stack([rotated(b[0:D], False), rotated(b[D:2 * D], False), rotated(b[0:D], True), rotated(b[D:2 * D], True)], axis=1)
    o["l3_wv"], o["l3_wo"], o["l3_bv"], o["l3_bo"] = w[:, None, 2 * D:], a["L3_attn_out_w"][:, None], b[None, 2 * D:], a["L3_attn_out_b"][None]
    for n, k in (("k0", 2), ("k1", 4), ("k2", 4)):
        fours = c(a[f"L3_ffn_{n}"]).view(np.int32)
        o[n] = fours.reshape(k, P, fours.shape[1]).transpose(1, 0, 2)
    o["s"] = np.stack([a["L3_ffn_s0"], a["L3_ffn_s1"], a["L3_ffn_s2"]])
    o["c_dft"], o["c_idft"], o["c_rotary"] = constants()
    return {k: c(v) for k, v in o.items()}


def kernel(**inputs):
    import concourse.bacc as bacc
    from concourse.bass_utils import run_bass_kernel_spmd

    arrays = lay_out(inputs)
    nc = bacc.Bacc("TRN2", target_bir_lowering=False, num_devices=1)
    a = {k: nc.dram_tensor(f"in_{k}", v.shape, mybir.dt.from_np(v.dtype), kind="ExternalInput").ap() for k, v in arrays.items()}
    out = nc.dram_tensor("out", (BATCHES * SEQ, D), F32, kind="ExternalOutput").ap()
    network(nc, a, out)
    r = run_bass_kernel_spmd(nc, [{f"in_{k}": v for k, v in arrays.items()}], core_ids=[0])
    return np.asarray(r.results[0]["out"]).reshape(BATCHES, SEQ, D)
```

```python
from contextlib import ExitStack

import numpy as np

import concourse.bass as bass
from concourse import mybir

F32 = mybir.dt.float32
BF16 = mybir.dt.bfloat16
I32 = mybir.dt.int32
U8 = mybir.dt.uint8
ALU = mybir.AluOpType
ACT = mybir.ActivationFunctionType
AX_X = mybir.AxisListType.X

P = 128
D = 128
BATCHES = 16
SEQ = 256
TILES = BATCHES * SEQ // P
GROUPS = 8
LN_EPS = 1e-5

HEADS = 16
HD = 8
SLOT = 32
BF_ROWS = 48
MASK_ROW = 64
MAX_ROW = 96
EXPERTS = 4

L0_HEADS = 16
L0_HD = 64
L0_PAIRS = L0_HEADS // 2
RMS_EPS = 1.1920929e-07

FREQS = D // 2 + 1
HIDDEN = 384
HCH = HIDDEN // P
FF3 = 512
NEG = -1e30


class Plan:

    def __init__(self, jobs, weights, unroll, first, rounds, drain, misc_uses=()):
        self.jobs, self.weights, self.unroll, self.first = jobs, weights, unroll, first
        self.rounds, self.drain, self.misc_uses = rounds, drain, misc_uses


class Weights:

    def __init__(self, wq=None, wk=None, wv=None, wo=None, bq=None, bk=None, bqk=None, bv=None, bo=None, bo_parts=None, wq2=None, wk2=None,
                 rot_bias=None, tables=None, router=None, router_b=None, exp_scale=1.0, ones_value=1.0,
                 gate=None, up=None, down=None, kqv=None, back=None, k0=None, k1=None, k2=None, s=None):
        self.wq, self.wk, self.wv, self.wo, self.bq, self.bk, self.bqk, self.bv, self.bo = wq, wk, wv, wo, bq, bk, bqk, bv, bo
        self.bo_parts, self.wq2, self.wk2, self.rot_bias, self.tables = bo_parts, wq2, wk2, rot_bias, tables
        self.router, self.router_b, self.exp_scale, self.ones_value = router, router_b, exp_scale, ones_value
        self.gate, self.up, self.down, self.kqv, self.back = gate, up, down, kqv, back
        self.k0, self.k1, self.k2, self.s = k0, k1, k2, s


class Model:

    def __init__(self, ctx):
        self.ctx = ctx


def stage(nc, ctx, name):
    held = []

    def sem(n):
        held.append(ctx.enter_context(nc.semaphore(f"{name}_{n}")))
        return held[-1]

    def sb(n, shape, dt=F32):
        return ctx.enter_context(nc.sbuf_tensor(f"{name}_{n}", shape, dt))

    def clear():
        with nc.Block() as block:
            @block.sync
            def _(sp):
                for h in held:
                    sp.sem_clear(h)

    def begin():
        ctx.callback(clear)
        return ctx.enter_context(nc.Block())

    return sem, sb, begin


def in_pairs(engine, group):
    for b in range(2):
        group(b, None)
    with engine.Fori(0, GROUPS // 2 - 1) as turns:
        for b in range(2):
            group(b, turns)


def batch_stats(dve, m, b):
    for t in range(2):
        last = dve.bn_stats(m.stats2[:, b, t, :], m.x32[:, b, t, :])
    return last


def group_stats(dve, m, g):
    for k in range(4):
        last = dve.bn_stats(m.stats4[:, g, k, :], m.x4[:, g, k, :])
    return last


def layer_norm(nc, m, name, rms=False, add_to_x=False, first=False, meanwhile=None):
    with ExitStack() as ctx:
        sem, sb, begin = stage(nc, ctx, name)
        stats = m.stats
        small = sb("small", [P, 8, TILES])
        xn = sb("xn", [P, 2, 4, D])
        turned = [ctx.enter_context(nc.psum_tensor(f"{name}_turned{k}", [P, 512], F32)) for k in range(2)]
        by_group = lambda a: a.rearrange("p (g k) -> p g k", k=4)
        mean, dif, var, root, rstd, tmp, guarded, shift = (small[:, k, :] for k in range(8))
        stats_done, dve_step, guarded_ready, root_ready = sem("stats_done"), sem("dve_step"), sem("guarded_ready"), sem("root_ready")
        xn_ready, turned_ready, xT_written, x_added = sem("xn_ready"), sem("turned_ready"), sem("xT_written"), sem("x_added")
        block = begin()

        if meanwhile:
            meanwhile(m, sem, block)

        @block.vector
        def _(dve):
            if first:
                with dve.Fori(0, GROUPS // 2) as r:
                    for k in range(8):
                        last = dve.bn_stats(stats[:, :, :].rearrange("p (r k) c -> p r k c", k=8)[:, r, k, :],
                                            m.x4[:, r * 2 + k // 4, k % 4, :])
                    last.then_inc(stats_done, 1)
                dve.wait_ge(stats_done, GROUPS // 2)
            n = [0]

            def then_wait(ins):
                n[0] += 1
                ins.then_inc(dve_step, 1)
                dve.wait_ge(dve_step, n[0])

            even, odd = stats[:, :, 1], stats[:, :, 4]
            dve.tensor_tensor(dif, even, odd, ALU.subtract).then_inc(dve_step, 1)
            dve.tensor_tensor(mean, even, odd, ALU.add).then_inc(dve_step, 1)
            n[0] = 2
            dve.wait_ge(dve_step, 2)
            dve.tensor_tensor(tmp, dif, dif, ALU.mult).then_inc(dve_step, 1)
            n[0] = 3
            then_wait(dve.tensor_tensor(var, stats[:, :, 2], stats[:, :, 5], ALU.add))
            then_wait(dve.scalar_tensor_tensor(out=var, in0=tmp, scalar=float(D // 4), in1=var, op0=ALU.mult, op1=ALU.add))
            if rms:
                then_wait(dve.tensor_scalar(guarded, var, (1.0 + RMS_EPS) / D, RMS_EPS * LN_EPS, ALU.mult, ALU.add))
            else:
                then_wait(dve.tensor_scalar(guarded, var, 1.0 / D, LN_EPS, ALU.mult, ALU.add))
            dve.tensor_scalar(mean, mean, 0.5, None, ALU.mult).then_inc(guarded_ready, 1)
            dve.wait_ge(guarded_ready, 1)
            dve.wait_ge(root_ready, 1)
            then_wait(dve.reciprocal(rstd, root))
            then_wait(dve.tensor_tensor(tmp, rstd, rstd, ALU.mult))
            then_wait(dve.tensor_tensor(tmp, tmp, guarded, ALU.mult))
            then_wait(dve.tensor_scalar(tmp, tmp, -0.5, 1.5, ALU.mult, ALU.add))
            then_wait(dve.tensor_tensor(rstd, rstd, tmp, ALU.mult))

            def group(b, turns):
                g = b if turns is None else turns * 2 + (b + 2)
                if turns is not None:
                    dve.wait_ge(turned_ready, turns * 2 + (b + 1))
                    if add_to_x:
                        dve.wait_ge(x_added, turns * 2 + (b + 1))
                for k in range(4):
                    last = dve.tensor_scalar(xn[:, b, k, :], m.x4[:, g, k, :], by_group(mean)[:, g, k:k + 1], by_group(rstd)[:, g, k:k + 1],
                                             ALU.subtract, ALU.mult)
                last.then_inc(xn_ready, 1)
                if add_to_x:
                    dve.wait_ge(xn_ready, b + 1 if turns is None else turns * 2 + (b + 3))
                    dve.tensor_tensor(m.xg[:, g, :], m.xg[:, g, :], xn[:, b, :, :].rearrange("p k d -> p (k d)"), ALU.add).then_inc(x_added, 1)

            in_pairs(dve, group)

        @block.scalar
        def _(act):
            act.wait_ge(dve_step, 6)
            act.activation(root, guarded, ACT.Sqrt).then_inc(root_ready, 1)
            with act.Fori(0, GROUPS // 2) as r:
                for b in range(2):
                    act.wait_ge(turned_ready, r * 2 + (b + 1))
                    act.activation(m.xT8[:, r * 2 + b, :], turned[b][:, :], ACT.Copy).then_inc(xT_written, 1)

        @block.tensor
        def _(pe):
            def group(b, turns):
                pe.wait_ge(xn_ready, b + 1 if turns is None else turns * 2 + (b + 3))
                if turns is not None:
                    pe.wait_ge(xT_written, turns * 2 + (b + 1))
                for k in range(4):
                    t = pe.transpose(turned[b][:, k * D:(k + 1) * D], xn[:, b, k, :], m.identity[:, :])
                t.then_inc(turned_ready, 1)

            in_pairs(pe, group)


class Step:

    def __init__(self, plan, at, turns):
        self.plan, self.at = plan, at
        self.turns = turns
        self.past = turns * plan.unroll if turns is not None else 0

    def has(self, off):
        return 0 <= self.at + off < self.plan.jobs

    def known(self, off, least=0):
        return self.at + off >= least

    def n(self, off, per=1, plus=0):
        return self.past * per + ((self.at + off) * per + plus)

    def parity(self, off):
        return (self.at + off) % 2

    def expert(self, off):
        return (self.at + off) % self.plan.weights

    def batch(self, off):
        b = (self.at + off) // self.plan.weights
        return b if self.turns is None else self.turns * (self.plan.unroll // self.plan.weights) + b

    def use(self, kind, off):
        uses = self.plan.misc_uses
        kinds = [k for k, _ in uses]
        mine = kinds.index(kind)
        step = self.at + off - uses[mine][1]
        n = sum(0 <= at + o < self.plan.jobs for at in range(-3, step) for _, o in uses)
        n += sum(0 <= step + o < self.plan.jobs for _, o in uses[:mine + 1])
        past = self.turns * (self.plan.unroll * len(uses) // 2) if self.turns is not None else 0
        return (n - 1) % 2, past + (n + 1) // 2


def wait_alone(engine, sem, value, passed):
    engine.wait_ge(sem, value)
    engine.sem_inc(passed, 1)


def pipeline(engine, plan, step):
    for at in range(-3, plan.first):
        step(Step(plan, at, None))
    with engine.Fori(0, plan.rounds) as turns:
        for u in range(plan.unroll):
            step(Step(plan, plan.first + u, turns))
    for at in range(plan.first + plan.rounds * plan.unroll, plan.jobs + plan.drain):
        step(Step(plan, at, None))


def attention8(nc, m, name, w, weights=1, rotary=False, masked=False, clear_mask=False):
    jobs, unroll, first = BATCHES * weights, max(2, weights), 4
    plan = Plan(jobs, weights, unroll, first, rounds=(jobs - 3 - first) // unroll, drain=1)
    plan.misc_uses = [("o2", -1), ("m1", 0), ("o3", -1), ("v", 1), ("y", -1), ("o0", 0), ("m0", 1), ("out", -1), ("o1", 0)]
    plan.misc_uses += [("qk", 3)] + ([("qk2", 3)] if rotary else [])

    with ExitStack() as ctx:
        sem, sb, begin = stage(nc, ctx, name)
        xcur = sb("xcur", [P, 2, SEQ])
        rest = sb("rest", [P, 2, SEQ])
        parts = sb("parts", [P, 2, 3, SEQ], BF16)
        stackq, stackk, values = m.stackq, m.stackk, m.values
        probs = sb("probs", [P, 2, 4, 2 * SEQ])
        rowmax = sb("rowmax", [P, 2, HEADS, 2])
        maxdif = sb("maxdif", [P, 2, 2, 8])
        negmax = sb("negmax", [P, 2, 2, 2, 8], BF16)
        negmaxT = sb("negmaxT", [16, 2, SEQ], BF16)
        oT = sb("oT", [P, 2, SEQ])
        rden = sb("rden", [P, 2, 2, 4])
        y = sb("y", [P, 2, D])
        yT = sb("yT", [P, SEQ])
        if rotary:
            turned = sb("turned", [P, 2, 2, SEQ])
            qk32 = sb("qk32", [P, 2, SEQ])
        psS = [ctx.enter_context(nc.psum_tensor(f"{name}_psS{k}", [P, 512], F32)) for k in range(2)]
        psT = [ctx.enter_context(nc.psum_tensor(f"{name}_psT{k}", [P, 512], F32)) for k in range(2)]
        psO = [ctx.enter_context(nc.psum_tensor(f"{name}_psO{k}", [P, 512], F32)) for k in range(2)]
        shared = [ctx.enter_context(nc.psum_tensor(f"{name}_shared{k}", [P, 512], F32)) for k in range(2)]
        scratch = nc.dram_tensor(f"{name}_scratch", (2, 2, 3, P, SEQ), BF16, kind="Internal").ap()

        stats_done = sem("stats_done")
        ones_set, mask_cleared, tokens_ready = sem("ones_set"), sem("mask_cleared"), sem("tokens_ready")
        sp_passed, pool_passed = sem("sp_passed"), sem("pool_passed")
        misc_full = [sem("misc_full0"), sem("misc_full1")]
        misc_taken = [sem("misc_taken0"), sem("misc_taken1")]
        high_ready, rest_ready, middle_ready, qk_summed = sem("high_ready"), sem("rest_ready"), sem("middle_ready"), sem("qk_summed")
        parts_ready, parts_saved = sem("parts_ready"), sem("parts_saved")
        stack_ready = [sem("stack_ready0"), sem("stack_ready1")]
        scores_ready, max_done = sem("scores_ready"), sem("max_done")
        negmax_step, negmax_ready = sem("negmax_step"), sem("negmax_ready")
        maxrow_ready = [sem("maxrow_ready0"), sem("maxrow_ready1")]
        shifted_ready, exp_done = sem("shifted_ready"), sem("exp_done")
        pv_ready, oT_ready, rden_ready = sem("pv_ready"), sem("oT_ready"), sem("rden_ready")
        stack_inc = 16 * (6 + (1 if masked else 0))

        def wait_taken(engine, s, kind, off):
            bank, count = s.use(kind, off)
            engine.wait_ge(misc_taken[bank], count)

        def wait_taken_alone(engine, s, kind, off, passed):
            bank, count = s.use(kind, off)
            wait_alone(engine, misc_taken[bank], count, passed)

        def wait_full(engine, s, kind, off):
            bank, count = s.use(kind, off)
            engine.wait_ge(misc_full[bank], count)
            return shared[bank], misc_taken[bank]

        block = begin()

        @block.sync
        def _(sp):
            if clear_mask:
                sp.dma_start(stackk[MASK_ROW:MASK_ROW + 1, :, :, :], stackk[BF_ROWS:BF_ROWS + 1, :, :, :]).then_inc(mask_cleared, 16)

            def max_rows(s, off, half):
                wait_taken_alone(sp, s, f"m{half}", off, sp_passed)
                for part in range(2):
                    sp.dma_start(stackq[MAX_ROW + part:MAX_ROW + part + 1, s.parity(off), 8 * half:8 * half + 8, :],
                                 negmaxT[8 * part:8 * part + 8, half, :]).then_inc(maxrow_ready[half], 16)

            def stack(s, half):
                b = s.parity(2)
                hs = slice(8 * half, 8 * half + 8)
                if s.known(2, 1):
                    wait_alone(sp, scores_ready, s.n(1, HEADS, 8 * half + 1), sp_passed)
                src = scratch[b].rearrange("qk part (d h) t -> qk part d h t", h=HEADS)
                for repeats, part, row in ((3, 0, 0), (2, 1, 24), (1, 2, 40)):
                    rows = slice(row, row + 8 * repeats)
                    sp.dma_start(stackq[rows, b, hs, :], src[0, part, :, hs, :].unsqueeze(0).to_broadcast([repeats, HD, 8, SEQ])).then_inc(stack_ready[half], 16)
                    sp.dma_start(stackk[rows, b, hs, :], src[1, 0:repeats, :, hs, :]).then_inc(stack_ready[half], 16)
                if masked:
                    row = m.mask_dram[s.batch(2), s.expert(2)]
                    sp.dma_start(stackk[MASK_ROW:MASK_ROW + 1, b, hs, :],
                                 row.unsqueeze(0).unsqueeze(0).to_broadcast([1, 8, SEQ])).then_inc(stack_ready[half], 16)

            def step(s):
                if s.has(0):
                    max_rows(s, 0, 1)
                if s.has(2):
                    wait_alone(sp, parts_ready, s.n(2, 1, 1), sp_passed)
                    if s.known(2, 2):
                        wait_alone(sp, stack_ready[1], s.n(2, stack_inc, -stack_inc), sp_passed)
                    sp.dma_start(scratch[s.parity(2)].rearrange("qk part p t -> p qk part t"),
                                 parts[:, :, :, :]).then_inc(parts_saved, 16)
                    wait_alone(sp, parts_saved, s.n(2, 16, 16), sp_passed)
                    if s.known(2, 2):
                        wait_alone(sp, shifted_ready, s.n(0, HEADS, 8), sp_passed)
                    stack(s, 0)
                if s.has(1):
                    max_rows(s, 1, 0)
                if s.has(2):
                    if s.known(2, 2):
                        wait_alone(sp, shifted_ready, s.n(0, HEADS, 16), sp_passed)
                    stack(s, 1)

            pipeline(sp, plan, step)

        @block.tensor
        def _(pe):
            pe.wait_ge(ones_set, 1)
            if clear_mask:
                pe.wait_ge(mask_cleared, 16)

            def fill(s, kind, off):
                bank, count = s.use(kind, off)
                if s.turns is not None or count > 1:
                    pe.wait_ge(misc_taken[bank], count - 1)
                return shared[bank], misc_full[bank]

            def project_qk(s, kind, wq, wk):
                pe.wait_ge(tokens_ready, s.n(3, 1, 1))
                ps, full = fill(s, kind, 3)
                xc = xcur[:, s.parity(3), :]
                pe.matmul(ps[:, 0:SEQ], wq[:, s.expert(3), :], xc, start=True, stop=True)
                pe.matmul(ps[:, SEQ:2 * SEQ], wk[:, s.expert(3), :], xc, start=True, stop=True).then_inc(full, 1)

            def project_v(s):
                ps, full = fill(s, "v", 1)
                for t in range(2):
                    mm = pe.matmul(ps[:, t * D:(t + 1) * D], xcur[:, s.parity(1), t * P:(t + 1) * P],
                                   w.wv[:, s.expert(1), :], start=True, stop=True)
                mm.then_inc(full, 1)

            def scores(s, h):
                if h % 8 == 0:
                    pe.wait_ge(stack_ready[h // 8], s.n(1, stack_inc, stack_inc))
                if s.known(1, 1) or h >= 2:
                    pe.wait_ge(max_done, s.n(1, HEADS, h - 1))
                b = s.parity(1)
                for t in range(2):
                    mm = pe.matmul(psS[h % 2][:, t * SEQ:(t + 1) * SEQ], stackq[0:MASK_ROW + 1, b, h, t * P:(t + 1) * P],
                                   stackk[0:MASK_ROW + 1, b, h, :], start=True, stop=True)
                mm.then_inc(scores_ready, 1)

            def shifted(s, h):
                if h % 8 == 0:
                    pe.wait_ge(maxrow_ready[h // 8], s.n(0, 32, 32))
                if s.known(0, 1) or h >= 2:
                    pe.wait_ge(exp_done, s.n(0, HEADS, h - 1))
                b = s.parity(0)
                for t in range(2):
                    mm = pe.matmul(psT[h % 2][:, t * SEQ:(t + 1) * SEQ],
                                   stackk[0:MAX_ROW + 2, b, h, t * P:(t + 1) * P],
                                   stackq[0:MAX_ROW + 2, b, h, :], start=True, stop=True)
                mm.then_inc(shifted_ready, 1)

            def prob_values(s, off, g):
                if g == 0:
                    wait_taken(pe, s, "v", off)
                pe.wait_ge(exp_done, s.n(off, HEADS, 4 * g + 4))
                if s.known(off, 1) or g >= 2:
                    pe.wait_ge(oT_ready, s.n(off, 4, g - 1))
                for t in range(2):
                    for j in range(4):
                        mm = pe.matmul(psO[g % 2][SLOT * j:SLOT * (j + 1), 0:SEQ], values[:, s.parity(off), t, 4 * g + j, :],
                                       probs[:, g % 2, j, t * SEQ:(t + 1) * SEQ], start=(t == 0), stop=(t == 1),
                                       tile_position=(0, SLOT * j), skip_group_check=True)
                mm.then_inc(pv_ready, 1)

            def turn_output(s, off, g):
                pe.wait_ge(oT_ready, s.n(off, 4, g + 1))
                ps, full = fill(s, f"o{g}", off)
                for t in range(2):
                    mm = pe.transpose(ps[:, t * P:(t + 1) * P], oT[:, g % 2, t * P:(t + 1) * P], m.identity[:, :])
                mm.then_inc(full, 1)

            def turn_max(s, off, half):
                pe.wait_ge(negmax_ready, s.n(off, 2, half + 1))
                ps, full = fill(s, f"m{half}", off)
                for t in range(2):
                    mm = pe.transpose(ps[0:16, 0:P].bitcast(BF16)[:, t * P:(t + 1) * P],
                                      negmax[:, half, t, :, :].rearrange("p a h -> p (a h)"), m.identity_bf[:, :])
                mm.then_inc(full, 1)

            def turn_y(s):
                wait_taken(pe, s, "o3", -1)
                ps, full = fill(s, "y", -1)
                for t in range(2):
                    mm = pe.transpose(ps[:, t * P:(t + 1) * P], y[:, t, :], m.identity[:, :])
                mm.then_inc(full, 1)

            def project_out(s):
                wait_taken(pe, s, "y", -1)
                ps, full = fill(s, "out", -1)
                e = s.expert(-1)
                for t in range(2):
                    for k in range(3):
                        pe.matmul(ps[:, t * D:(t + 1) * D], m.ones_bf[:, 0:P], w.bo_parts[:, k, e, :], start=(k == 0), stop=False)
                    mm = pe.matmul(ps[:, t * D:(t + 1) * D], yT[:, t * P:(t + 1) * P], w.wo[:, e, :], start=False, stop=True)
                mm.then_inc(full, 1)

            def step(s):
                for h in range(HEADS):
                    if s.has(1):
                        scores(s, h)
                    if s.has(0):
                        shifted(s, h)
                    if h == 1 and s.has(-1):
                        turn_output(s, -1, 2)
                    if h == 2 and s.has(-1):
                        prob_values(s, -1, 3)
                    if h == 4 and s.has(0):
                        turn_max(s, 0, 1)
                    if h == 5 and s.has(-1):
                        turn_output(s, -1, 3)
                    if h in (6, 10, 14) and s.has(0):
                        prob_values(s, 0, (h - 6) // 4)
                    if h == 7 and s.has(1):
                        project_v(s)
                    if h == 8 and s.has(-1):
                        turn_y(s)
                    if h == 9 and s.has(0):
                        turn_output(s, 0, 0)
                    if h == 10 and s.has(1):
                        turn_max(s, 1, 0)
                    if h == 12 and s.has(-1):
                        project_out(s)
                    if h == 13 and s.has(0):
                        turn_output(s, 0, 1)
                    if h == 15 and s.has(3):
                        project_qk(s, "qk", w.wq, w.wk)
                        if rotary:
                            project_qk(s, "qk2", w.wq2, w.wk2)

            pipeline(pe, plan, step)

        @block.scalar
        def _(act):
            def high_part(s):
                if s.known(2, 1):
                    act.wait_ge(parts_saved, s.n(2, 16))
                if rotary:
                    act.wait_ge(qk_summed, s.n(2, 1, 1))
                    act.activation(parts[:, :, 0, :], qk32[:, :, :], ACT.Copy).then_inc(high_ready, 1)
                else:
                    ps, _ = wait_full(act, s, "qk", 2)
                    e = s.expert(2)
                    act.activation(parts[:, 0, 0, :], ps[:, 0:SEQ], ACT.Identity, bias=w.bq[:, e:e + 1])
                    act.activation(parts[:, 1, 0, :], ps[:, SEQ:2 * SEQ], ACT.Identity, bias=w.bk[:, e:e + 1]).then_inc(high_ready, 1)

            def exponential(s, h):
                act.wait_ge(shifted_ready, s.n(0, HEADS, h + 1))
                if h % 4 == 0 and (s.known(0, 1) or h >= 8):
                    act.wait_ge(pv_ready, s.n(0, 4, h // 4 - 1))
                act.activation(probs[:, h // 4 % 2, h % 4, :], psT[h % 2][:, :], ACT.Exp, scale=w.exp_scale).then_inc(exp_done, 1)

            def copy_oT(s, off, g):
                act.wait_ge(pv_ready, s.n(off, 4, g + 1))
                if g >= 2:
                    wait_taken(act, s, f"o{g - 2}", off)
                elif s.known(off, 1):
                    wait_taken(act, s, f"o{g + 2}", off - 1)
                act.activation(oT[:, g % 2, :], psO[g % 2][:, 0:SEQ], ACT.Copy).then_inc(oT_ready, 1)

            def copy_max(s, off, half):
                ps, taken = wait_full(act, s, f"m{half}", off)
                if s.known(off, 1):
                    act.wait_ge(maxrow_ready[half], s.n(off, 32))
                act.activation(negmaxT[:, half, :], ps[0:16, 0:P].bitcast(BF16), ACT.Copy).then_inc(taken, 1)

            def copy_yT(s):
                ps, taken = wait_full(act, s, "y", -1)
                if s.known(-1, 1):
                    wait_taken(act, s, "out", -2)
                act.activation(yT[:, :], ps[:, 0:SEQ], ACT.Copy).then_inc(taken, 1)

            def step(s):
                for h in range(HEADS):
                    if h == (2 if rotary else 0) and s.has(2):
                        high_part(s)
                    if h == 3 and s.has(-1):
                        copy_oT(s, -1, 3)
                    if h == 4 and s.has(0):
                        copy_max(s, 0, 1)
                    if h == 8 and s.has(-1):
                        copy_yT(s)
                    if h == 11 and s.has(1):
                        copy_max(s, 1, 0)
                    if s.has(0):
                        exponential(s, h)
                    if h in (7, 11, 15) and s.has(0):
                        copy_oT(s, 0, (h - 7) // 4)

            pipeline(act, plan, step)

        @block.vector
        def _(dve):
            dve.memset(values[:, :, :, :, HD:HD + 1], w.ones_value).then_inc(ones_set, 1)

            def rest_of_high(s):
                ps, taken = wait_full(dve, s, "qk", 2)
                dve.wait_ge(high_ready, s.n(2, 1, 1))
                for k, bias in enumerate((w.bq, w.bk)):
                    r = dve.scalar_tensor_tensor(out=rest[:, k, :], in0=ps[:, k * SEQ:(k + 1) * SEQ], scalar=bias[:, s.expert(2):s.expert(2) + 1],
                                                 in1=parts[:, k, 0, :], op0=ALU.add, op1=ALU.subtract)
                r.then_inc(taken, 1)

            def rotary_half(s, kind, which):
                ps, taken = wait_full(dve, s, kind, 3)
                if which == 0 and s.known(3, 1):
                    dve.wait_ge(qk_summed, s.n(3))
                for k in range(2):
                    t = dve.scalar_tensor_tensor(out=turned[:, which, k, :], in0=ps[:, k * SEQ:(k + 1) * SEQ],
                                                 scalar=w.rot_bias[:, 2 * which + k:2 * which + k + 1], in1=w.tables[:, which, k, :],
                                                 op0=ALU.add, op1=ALU.mult)
                t.then_inc(taken, 1)

            def maxima(s, h):
                dve.wait_ge(scores_ready, s.n(1, HEADS, h + 1))
                if h % 8 == 0 and s.known(1, 2):
                    dve.wait_ge(negmax_ready, s.n(1, 2, h // 8 - 3))
                dve.tensor_reduce(rowmax[:, s.parity(1), h, :], psS[h % 2][:, :].rearrange("p (t k) -> p t k", t=2),
                                  AX_X, ALU.max).then_inc(max_done, 1)

            def write_values(s):
                ps, taken = wait_full(dve, s, "v", 1)
                if s.known(1, 2):
                    dve.wait_ge(pv_ready, s.n(1, 4, -4))
                dve.tensor_tensor(values[:, s.parity(1), :, :, 0:HD], ps[:, 0:2 * D].rearrange("p (t h d) -> p t h d", t=2, d=HD),
                                  w.bv[:, s.expert(1), :].rearrange("p (h d) -> p h d", d=HD).unsqueeze(1).to_broadcast([P, 2, HEADS, HD]),
                                  ALU.add).then_inc(taken, 1)

            def normalise(s, off, g):
                ps, taken = wait_full(dve, s, f"o{g}", off)
                if g == 0 and s.known(off, 1):
                    wait_taken(dve, s, "y", off - 1)
                o = ps[:, 0:SEQ].rearrange("p (t j c) -> p t j c", t=2, c=SLOT)
                dve.reciprocal(rden[:, g % 2, :, :], o[:, :, :, HD]).then_inc(rden_ready, 1)
                dve.wait_ge(rden_ready, s.n(off, 4, g + 1))
                dve.tensor_tensor(y[:, :, 4 * HD * g:4 * HD * (g + 1)].rearrange("p t (j d) -> p t j d", d=HD), o[:, :, :, 0:HD],
                                  rden[:, g % 2, :, :].unsqueeze(3).to_broadcast([P, 2, 4, HD]), ALU.mult).then_inc(taken, 1)

            def add_output(s):
                ps, taken = wait_full(dve, s, "out", -1)
                if s.known(-1, 1):
                    wait_taken(dve, s, "out", -2)
                b, e = s.batch(-1), s.expert(-1)
                if masked:
                    for t in range(2):
                        u = dve.scalar_tensor_tensor(out=m.x32[:, b, t, :], in0=ps[:, t * D:(t + 1) * D],
                                                     scalar=m.gate[:, b, t, e:e + 1], in1=m.x32[:, b, t, :],
                                                     op0=ALU.mult, op1=ALU.add)
                else:
                    u = dve.tensor_tensor(m.x16[:, b, :], ps[:, 0:SEQ], m.x16[:, b, :], ALU.add)
                u.then_inc(taken, 1)

            def output_stats(s):
                wait_taken(dve, s, "out", -1)
                batch_stats(dve, m, s.batch(-1)).then_inc(stats_done, 1)

            def step(s):
                for h in range(HEADS):
                    if s.has(1):
                        maxima(s, h)
                    if h == 0 and s.has(2) and not rotary:
                        rest_of_high(s)
                    if h == 15 and s.has(3) and rotary:
                        rotary_half(s, "qk", 0)
                        rotary_half(s, "qk2", 1)
                    if h == 2 and s.has(-1):
                        normalise(s, -1, 2)
                    if h == 6 and s.has(-1):
                        normalise(s, -1, 3)
                    if h == 7 and s.has(1):
                        write_values(s)
                    if h == 10 and s.has(0):
                        normalise(s, 0, 0)
                    if h == 12 and s.has(-1):
                        add_output(s)
                    if h == 13 and s.has(-1) and s.expert(-1) == weights - 1:
                        output_stats(s)
                    if h == 14 and s.has(0):
                        normalise(s, 0, 1)

            pipeline(dve, plan, step)

        @block.gpsimd
        def _(pool):
            def tokens(s):
                if s.known(3, 2):
                    wait_taken_alone(pool, s, "v", 1, pool_passed)
                pool.tensor_copy(xcur[:, s.parity(3), :], m.xT16[:, s.batch(3), :]).then_inc(tokens_ready, 1)

            def sum_rotary(s):
                wait_taken_alone(pool, s, "qk2", 2, pool_passed)
                if s.known(2, 1):
                    wait_alone(pool, high_ready, s.n(2), pool_passed)
                    wait_alone(pool, rest_ready, s.n(2), pool_passed)
                pool.tensor_tensor(qk32[:, :, :], turned[:, 0, :, :], turned[:, 1, :, :], ALU.add).then_inc(qk_summed, 1)

            def split(s):
                if rotary:
                    wait_alone(pool, high_ready, s.n(2, 1, 1), pool_passed)
                    pool.tensor_tensor(rest[:, :, :], qk32[:, :, :], parts[:, :, 0, :], ALU.subtract).then_inc(rest_ready, 1)
                    wait_alone(pool, rest_ready, s.n(2, 1, 1), pool_passed)
                else:
                    wait_taken_alone(pool, s, "qk", 2, pool_passed)
                pool.tensor_copy(parts[:, :, 1, :], rest[:, :, :]).then_inc(middle_ready, 1)
                wait_alone(pool, middle_ready, s.n(2, 1, 1), pool_passed)
                pool.tensor_tensor(parts[:, :, 2, :], rest[:, :, :], parts[:, :, 1, :], ALU.subtract).then_inc(parts_ready, 1)

            def split_max(s, half):
                wait_alone(pool, max_done, s.n(1, HEADS, 8 * half + 8), pool_passed)
                if s.known(1, 1):
                    wait_taken_alone(pool, s, f"m{half}", 0, pool_passed)
                mx = rowmax[:, s.parity(1), 8 * half:8 * half + 8, :].rearrange("p h t -> p t h")
                pool.tensor_scalar(negmax[:, half, :, 0, :], mx, -1.0, None, ALU.mult).then_inc(negmax_step, 1)
                wait_alone(pool, negmax_step, s.n(1, 4, 2 * half + 1), pool_passed)
                pool.tensor_tensor(maxdif[:, half, :, :], mx, negmax[:, half, :, 0, :], ALU.add).then_inc(negmax_step, 1)
                wait_alone(pool, negmax_step, s.n(1, 4, 2 * half + 2), pool_passed)
                pool.tensor_scalar(negmax[:, half, :, 1, :], maxdif[:, half, :, :], -1.0, None, ALU.mult).then_inc(negmax_ready, 1)

            def step(s):
                if s.has(2):
                    if rotary:
                        sum_rotary(s)
                    split(s)
                if s.has(1):
                    split_max(s, 0)
                if s.has(3):
                    tokens(s)
                if s.has(1):
                    split_max(s, 1)

            pipeline(pool, plan, step)


def attention64(nc, m, w):
    jobs = BATCHES * L0_PAIRS
    plan = Plan(jobs=jobs, weights=L0_PAIRS, unroll=L0_PAIRS, first=L0_PAIRS + 2,
                           rounds=BATCHES - 2, drain=2)
    with ExitStack() as ctx:
        sem, sb, begin = stage(nc, ctx, "a64")
        xcur = sb("xcur", [P, SEQ])
        qT = sb("qT", [P, 2, SEQ])
        kT = sb("kT", [P, 2, 2, SEQ])
        v = sb("v", [P, 2, 4, L0_HD])
        vr = sb("vr", [P, 2, 4, L0_HD])
        probs = sb("probs", [P, 2, 2, 384])
        negmax = sb("negmax", [P, 2, 4])
        sums = sb("sums", [P, 2, 4])
        rsum = sb("rsum", [P, 2, 4])
        zT = sb("zT", [P, 2, SEQ])
        pb = lambda n: ctx.enter_context(nc.psum_tensor(f"a64_{n}", [P, 512], F32))
        psQ, psV, psZ, psX = pb("psQ"), pb("psV"), pb("psZ"), pb("psX")
        psS = [[pb(f"psS{a}{h}") for h in range(2)] for a in range(2)]
        preset, tokens_ready = sem("preset"), sem("tokens_ready")
        qk_projected, q_ready, k_ready = sem("qk_projected"), sem("q_ready"), sem("k_ready")
        v_projected, v_ready, scores_ready, negmax_ready = sem("v_projected"), sem("v_ready"), sem("scores_ready"), sem("negmax_ready")
        exp_done, rsum_ready, vr_ready = sem("exp_done"), sem("rsum_ready"), sem("vr_ready")
        pv_ready, zT_ready, out_done, x_updated = sem("pv_ready"), sem("zT_ready"), sem("out_done"), sem("x_updated")
        out_step, pool_passed, stats_done = sem("out_step"), sem("pool_passed"), sem("stats_done")
        block = begin()

        @block.sync
        def _(sp):
            for dst, src in m.later_loads:
                sp.dma_start(dst, src).then_inc(m.rest_loaded, 16)

        @block.gpsimd
        def _(pool):
            pool.memset(kT[:, :, :, :], 0.0).then_inc(preset, 1)

            def step(s):
                if s.has(2) and (s.at + 2) % L0_PAIRS == 0:
                    if s.known(2, 1):
                        wait_alone(pool, v_projected, s.n(2), pool_passed)
                    pool.tensor_copy(xcur[:, :], m.xT16[:, s.batch(2), :]).then_inc(tokens_ready, 1)
                if s.has(-1):
                    wait_alone(pool, rsum_ready, s.n(-1, 1, 1), pool_passed)
                    if s.known(-1, 2):
                        wait_alone(pool, pv_ready, s.n(-1, 1, -1), pool_passed)
                    pool.tensor_tensor(vr[:, s.parity(-1), :, :], v[:, s.parity(-1), :, :],
                                       rsum[:, s.parity(-1), :].unsqueeze(2).to_broadcast([P, 4, L0_HD]), ALU.mult).then_inc(vr_ready, 1)

            pipeline(pool, plan, step)

        @block.tensor
        def _(pe):
            pe.wait_ge(preset, 1)
            pe.wait_ge(m.l0_loaded, m.l0_loads)

            def scores(s, h):
                a = s.parity(0)
                if h == 0:
                    pe.wait_ge(q_ready, s.n(0, 1, 1))
                    pe.wait_ge(k_ready, s.n(0, 1, 1))
                if s.known(0, 2):
                    pe.wait_ge(exp_done, s.n(0, 2, h - 3))
                ps = psS[a][h]
                pe.matmul(ps[:, 0:P], m.identity_bf[:, :], m.causal[:, :], start=True, stop=False, skip_group_check=True)
                pe.matmul(ps[:, 0:SEQ], kT[:, a, h, 0:P], qT[:, a, :], start=False, stop=True, skip_group_check=True)
                pe.matmul(ps[:, SEQ:384], kT[:, a, h, P:SEQ], qT[:, a, P:SEQ], start=True, stop=False, skip_group_check=True)
                pe.matmul(ps[:, SEQ:384], m.identity_bf[:, :], m.causal[:, :], start=False, stop=True, skip_group_check=True).then_inc(scores_ready, 1)

            def project(s):
                p = s.expert(1)
                if p == 0:
                    pe.wait_ge(tokens_ready, s.batch(1) + 1)
                if s.known(1, 1):
                    pe.wait_ge(q_ready, s.n(1))
                    pe.wait_ge(k_ready, s.n(1))
                pe.matmul(psQ[:, 0:SEQ], w.wq[:, p * P:(p + 1) * P], xcur[:, :], start=True, stop=True)
                pe.matmul(psQ[:, SEQ:512], w.wk[:, p * P:(p + 1) * P], xcur[:, :], start=True, stop=True).then_inc(qk_projected, 1)
                if s.known(1, 1):
                    pe.wait_ge(v_ready, s.n(1))
                for t in range(2):
                    mm = pe.matmul(psV[:, t * P:(t + 1) * P], xcur[:, t * P:(t + 1) * P], w.wv[:, p * P:(p + 1) * P], start=True, stop=True)
                mm.then_inc(v_projected, 1)

            def prob_values(s):
                b = s.parity(-1)
                pe.wait_ge(vr_ready, s.n(-1, 1, 1))
                if s.known(-1, 1):
                    pe.wait_ge(zT_ready, s.n(-1))
                for h in range(2):
                    pe.matmul(psZ[64 * h:64 * h + 64, P:SEQ], vr[:, b, 2 * h + 1, :], probs[:, b, h, SEQ:384], start=True, stop=False,
                              tile_position=(0, 64 * h), skip_group_check=True)
                for h in range(2):
                    mm = pe.matmul(psZ[64 * h:64 * h + 64, 0:SEQ], vr[:, b, 2 * h, :], probs[:, b, h, 0:SEQ], start=False, stop=True,
                                   tile_position=(0, 64 * h), skip_group_check=True)
                mm.then_inc(pv_ready, 1)

            def project_out(s):
                p, b = s.expert(-2), s.parity(-2)
                pe.wait_ge(zT_ready, s.n(-2, 1, 1))
                if p == 0 and s.at - 2 >= L0_PAIRS:
                    pe.wait_ge(x_updated, s.batch(-2))
                for t in range(2):
                    mm = pe.matmul(psX[:, t * D:(t + 1) * D], zT[:, b, t * P:(t + 1) * P], w.wo[:, p, :],
                                   start=(p == 0 and t == 0), stop=False, skip_group_check=True)
                mm.then_inc(out_step, 1)
                if p == L0_PAIRS - 1:
                    for t in range(2):
                        mm = pe.matmul(psX[:, t * D:(t + 1) * D], m.ones[:, :], w.bo[:, :], start=False, stop=True, skip_group_check=True)
                    mm.then_inc(out_done, 1)

            def step(s):
                if s.has(0):
                    scores(s, 0)
                if s.has(1):
                    project(s)
                if s.has(0):
                    scores(s, 1)
                if s.has(-2):
                    project_out(s)
                if s.has(-1):
                    prob_values(s)

            pipeline(pe, plan, step)

        @block.scalar
        def _(act):
            act.wait_ge(m.l0_loaded, m.l0_loads)

            def step(s):
                if s.has(1):
                    act.wait_ge(qk_projected, s.n(1, 1, 1))
                    if s.known(1, 2):
                        act.wait_ge(scores_ready, s.n(1, 2, -2))
                    p = s.expert(1)
                    act.activation(qT[:, s.parity(1), :], psQ[:, 0:SEQ], ACT.Identity, bias=w.bqk[:, p, 0:1]).then_inc(q_ready, 1)
                if s.has(0):
                    a = s.parity(0)
                    for h in range(2):
                        act.wait_ge(negmax_ready, s.n(0, 2, h + 1))
                        if h == 0 and s.known(0, 2):
                            act.wait_ge(pv_ready, s.n(0, 1, -1))
                        act.activation(probs[:, a, h, 0:SEQ], psS[a][h][:, 0:SEQ], ACT.Exp, bias=negmax[:, a, 2 * h:2 * h + 1],
                                       accum_out=sums[:, a, 2 * h:2 * h + 1])
                        act.activation(probs[:, a, h, SEQ:384], psS[a][h][:, SEQ:384], ACT.Exp, bias=negmax[:, a, 2 * h + 1:2 * h + 2],
                                       accum_out=sums[:, a, 2 * h + 1:2 * h + 2]).then_inc(exp_done, 1)
                if s.has(-1):
                    act.wait_ge(pv_ready, s.n(-1, 1, 1))
                    if s.known(-1, 2):
                        act.wait_ge(out_step, s.n(-1, 1, -1))
                    act.activation(zT[:, s.parity(-1), :], psZ[:, 0:SEQ], ACT.Copy).then_inc(zT_ready, 1)

            pipeline(act, plan, step)

        @block.vector
        def _(dve):
            dve.wait_ge(preset, 1)
            dve.wait_ge(m.l0_loaded, m.l0_loads)

            def step(s):
                if s.has(0):
                    a = s.parity(0)
                    for h in range(2):
                        dve.wait_ge(scores_ready, s.n(0, 2, h + 1))
                        if s.known(0, 2):
                            dve.wait_ge(exp_done, s.n(0, 2, h - 3))
                        dve.tensor_reduce(negmax[:, a, 2 * h:2 * h + 1], psS[a][h][:, 0:SEQ], AX_X, ALU.max, negate=True)
                        dve.tensor_reduce(negmax[:, a, 2 * h + 1:2 * h + 2], psS[a][h][:, SEQ:384], AX_X, ALU.max,
                                          negate=True).then_inc(negmax_ready, 1)
                        if h == 0 and s.has(1):
                            take_kv(s)
                if s.has(1) and not s.has(0):
                    take_kv(s)
                if s.has(0):
                    dve.wait_ge(exp_done, s.n(0, 2, 2))
                    if s.known(0, 2):
                        dve.wait_ge(vr_ready, s.n(0, 1, -1))
                    dve.reciprocal(rsum[:, s.parity(0), :], sums[:, s.parity(0), :]).then_inc(rsum_ready, 1)
                if s.has(-2) and s.expert(-2) == L0_PAIRS - 1:
                    b = s.batch(-2)
                    dve.wait_ge(out_done, b + 1)
                    dve.tensor_tensor(m.x16[:, b, :], psX[:, 0:SEQ], m.x16[:, b, :], ALU.add).then_inc(x_updated, 1)
                    dve.wait_ge(x_updated, b + 1)
                    batch_stats(dve, m, b).then_inc(stats_done, 1)

            def take_kv(s):
                c, p = s.parity(1), s.expert(1)
                dve.wait_ge(q_ready, s.n(1, 1, 1))
                for h in range(2):
                    r = slice(64 * h, 64 * h + 64)
                    k = dve.tensor_scalar(kT[r, c, h, :], psQ[r, SEQ:512], w.bqk[r, p, 1:2], None, ALU.add)
                k.then_inc(k_ready, 1)
                dve.wait_ge(v_projected, s.n(1, 1, 1))
                if s.known(1, 2):
                    dve.wait_ge(vr_ready, s.n(1, 1, -1))
                dve.tensor_tensor(v[:, c, :, :].rearrange("p (h t) d -> p t h d", h=2),
                                  psV[:, 0:SEQ].rearrange("p (t h d) -> p t h d", t=2, h=2),
                                  w.bv[:, p * P:(p + 1) * P].rearrange("p (h d) -> p h d", h=2).unsqueeze(1).to_broadcast([P, 2, 2, L0_HD]),
                                  ALU.add).then_inc(v_ready, 1)

            pipeline(dve, plan, step)


def swiglu(nc, m, name, w):
    with ExitStack() as ctx:
        sem, sb, begin = stage(nc, ctx, name)
        silu = sb("silu", [P, 2, 512])
        hidden = sb("hidden", [P, 2, HCH, 512])
        pb = lambda n: ctx.enter_context(nc.psum_tensor(f"{name}_{n}", [P, 512], F32))
        gate, up, out = [pb("gate0"), pb("gate1")], [pb("up0"), pb("up1")], [pb("out0"), pb("out1")]
        projected, silu_ready, hidden_ready, out_ready, x_updated = (
            sem("projected"), sem("silu_ready"), sem("hidden_ready"), sem("out_ready"), sem("x_updated"))
        stats_done = sem("stats_done")
        block = begin()
        plan = Plan(jobs=GROUPS, weights=1, unroll=2, first=2, rounds=(GROUPS - 3) // 2, drain=1)

        def bank(s, c):
            return (s.at * HCH + c) % 2

        @block.tensor
        def _(pe):
            def step(s):
                for c in range(HCH):
                    if s.has(0):
                        if s.known(0, 1) or c >= 2:
                            pe.wait_ge(hidden_ready, s.n(0, HCH, c - 1))
                        b, g = bank(s, c), s.batch(0)
                        pe.matmul(gate[b][:, :], w.gate[:, c * P:(c + 1) * P], m.xT8[:, g, :], start=True, stop=True)
                        pe.matmul(up[b][:, :], w.up[:, c * P:(c + 1) * P], m.xT8[:, g, :], start=True, stop=True).then_inc(projected, 1)
                    if c == 0 and s.has(-1):
                        h = s.parity(-1)
                        pe.wait_ge(hidden_ready, s.n(-1, HCH, HCH))
                        if s.known(-1, 2):
                            pe.wait_ge(x_updated, s.n(-1, 1, -1))
                        for t in range(4):
                            for k in range(HCH):
                                mm = pe.matmul(out[h][:, t * D:(t + 1) * D], hidden[:, h, k, t * P:(t + 1) * P], w.down[:, k, :],
                                               start=(k == 0), stop=(k == HCH - 1))
                        mm.then_inc(out_ready, 1)

            pipeline(pe, plan, step)

        @block.scalar
        def _(act):
            def step(s):
                if s.has(0):
                    for c in range(HCH):
                        act.wait_ge(projected, s.n(0, HCH, c + 1))
                        if s.known(0, 1) or c >= 2:
                            act.wait_ge(hidden_ready, s.n(0, HCH, c - 1))
                        b = bank(s, c)
                        act.activation(silu[:, b, :], gate[b][:, :], ACT.Silu).then_inc(silu_ready, 1)

            pipeline(act, plan, step)

        @block.vector
        def _(dve):
            def step(s):
                for c in range(HCH):
                    if s.has(0):
                        b = bank(s, c)
                        dve.wait_ge(silu_ready, s.n(0, HCH, c + 1))
                        if c == 0 and s.known(0, 2):
                            dve.wait_ge(out_ready, s.n(0, 1, -1))
                        dve.tensor_tensor(hidden[:, s.parity(0), c, :], silu[:, b, :], up[b][:, :], ALU.mult).then_inc(hidden_ready, 1)
                    if c == 1 and s.has(-1):
                        g = s.batch(-1)
                        dve.wait_ge(out_ready, s.n(-1, 1, 1))
                        dve.tensor_tensor(m.xg[:, g, :], out[s.parity(-1)][:, :], m.xg[:, g, :], ALU.add).then_inc(x_updated, 1)
                    if c == 2 and s.has(-1):
                        dve.wait_ge(x_updated, s.n(-1, 1, 1))
                        group_stats(dve, m, s.batch(-1)).then_inc(stats_done, 1)

            pipeline(dve, plan, step)


def sign_mlp(nc, m, w):
    CH = FF3 // P
    with ExitStack() as ctx:
        sem, sb, begin = stage(nc, ctx, "mlp")
        h0 = sb("h0", [P, 2, CH, 512])
        h1 = sb("h1", [P, CH, 512])
        pb = lambda n: ctx.enter_context(nc.psum_tensor(f"mlp_{n}", [P, 512], F32))
        banks0, banks1, out = [pb("a0"), pb("a1")], [pb("b0"), pb("b1")], [pb("out0"), pb("out1")]
        p0, h0_ready, p1, h1_ready, out_ready, x_updated = (sem("p0"), sem("h0_ready"), sem("p1"), sem("h1_ready"), sem("out_ready"), sem("x_updated"))
        block = begin()
        plan = Plan(jobs=GROUPS, weights=1, unroll=2, first=2, rounds=(GROUPS - 4) // 2, drain=1)

        @block.tensor
        def _(pe):
            def step(s):
                for c in range(CH):
                    if s.has(1):
                        if s.known(1, 1) or c >= 2:
                            pe.wait_ge(h0_ready, s.n(1, CH, c - 1))
                        pe.matmul(banks0[c % 2][:, :], w.k0[:, c * P:(c + 1) * P], m.xT8[:, s.batch(1), :], start=True, stop=True).then_inc(p0, 1)
                    if c == 1 and s.has(-1):
                        pe.wait_ge(h1_ready, s.n(-1, CH, CH))
                        if s.known(-1, 2):
                            pe.wait_ge(x_updated, s.n(-1, 1, -1))
                        for t in range(4):
                            for k in range(CH):
                                mm = pe.matmul(out[s.parity(-1)][:, t * D:(t + 1) * D], h1[:, k, t * P:(t + 1) * P], w.k2[:, k, :],
                                               start=(k == 0), stop=(k == CH - 1))
                        mm.then_inc(out_ready, 1)
                    if s.has(0):
                        if c == 0:
                            pe.wait_ge(h0_ready, s.n(0, CH, CH))
                        if s.known(0, 1) or c >= 2:
                            pe.wait_ge(h1_ready, s.n(0, CH, c - 1))
                        for k in range(CH):
                            mm = pe.matmul(banks1[c % 2][:, :], w.k1[:, k, c * P:(c + 1) * P], h0[:, s.parity(0), k, :],
                                           start=(k == 0), stop=(k == CH - 1))
                        mm.then_inc(p1, 1)

            pipeline(pe, plan, step)

        @block.scalar
        def _(act):
            def step(s):
                for c in range(CH):
                    if s.has(1):
                        act.wait_ge(p0, s.n(1, CH, c + 1))
                        if c == 0 and s.known(1, 2):
                            act.wait_ge(p1, s.n(1, CH, -CH))
                        act.activation(h0[:, s.parity(1), c, :], banks0[c % 2][:, :], ACT.Relu, scale=w.s[:, 0:1]).then_inc(h0_ready, 1)

            pipeline(act, plan, step)

        @block.vector
        def _(dve):
            def step(s):
                for c in range(CH):
                    if c == 2 and s.has(-1):
                        g = s.batch(-1)
                        dve.wait_ge(out_ready, s.n(-1, 1, 1))
                        dve.scalar_tensor_tensor(out=m.xg[:, g, :], in0=out[s.parity(-1)][:, :], scalar=w.s[:, 2:3], in1=m.xg[:, g, :],
                                                 op0=ALU.mult, op1=ALU.add).then_inc(x_updated, 1)
                    if s.has(0):
                        dve.wait_ge(p1, s.n(0, CH, c + 1))
                        if c == 0 and s.known(0, 1):
                            dve.wait_ge(out_ready, s.n(0))
                        dve.tensor_scalar(h1[:, c, :], banks1[c % 2][:, :], w.s[:, 1:2], 0.0, ALU.mult, ALU.max).then_inc(h1_ready, 1)

            pipeline(dve, plan, step)


def fourier_attention(nc, m, w):
    F2 = 2 * FREQS
    with ExitStack() as ctx:
        sem, sb, begin = stage(nc, ctx, "fft")
        xcur = sb("xcur", [P, 2, SEQ])
        kqv = sb("kqv", [P, 2, 2, 3 * F2])
        square = sb("square", [P, 2, 2 * F2])
        power = sb("power", [P, 2, 2, FREQS])
        size = sb("size", [P, 2, 2, FREQS])
        inverse = sb("inverse", [P, 2, 2, FREQS])
        prod = sb("prod", [P, 2, F2])
        cross = sb("cross", [P, 2, 2, FREQS])
        kv = sb("kv", [P, 2, 2, F2])
        qT = sb("qT", [FREQS, 2, SEQ])
        total = sb("total", [FREQS, 2, SEQ])
        straight = sb("straight", [FREQS, 2, SEQ])
        across = sb("across", [FREQS, 2, SEQ])
        final = sb("final", [FREQS, 2, SEQ])
        pb = lambda n: ctx.enter_context(nc.psum_tensor(f"fft_{n}", [P, 512], F32))
        psP, psQ, psC, psX = [pb("psP0"), pb("psP1")], pb("psQ"), pb("psC"), pb("psX")
        tokens_ready, projected, kqv_ready, dve_step, power_ready, size_ready = (
            sem("tokens_ready"), sem("projected"), sem("kqv_ready"), sem("dve_step"), sem("power_ready"), sem("size_ready"))
        unit_ready, kv_ready, q_turned, qT_ready, total_ready, total_copied, final_ready, out_ready, x_updated = (
            sem("unit_ready"), sem("kv_ready"), sem("q_turned"), sem("qT_ready"), sem("total_ready"), sem("total_copied"),
            sem("final_ready"), sem("out_ready"), sem("x_updated"))
        pool_passed, across_ready, stats_done = sem("pool_passed"), sem("across_ready"), sem("stats_done")
        block = begin()
        plan = Plan(jobs=BATCHES, weights=1, unroll=2, first=3, rounds=(BATCHES - 6) // 2, drain=0)
        K, Q, V = (slice(i * F2, (i + 1) * F2) for i in range(3))

        def halves(a):
            return a.rearrange("p t (c f) -> p t c f", c=2)

        @block.gpsimd
        def _(pool):
            def step(s):
                if s.has(3):
                    if s.known(3, 2):
                        wait_alone(pool, projected, s.n(1, 1, 1), pool_passed)
                    pool.tensor_copy(xcur[:, s.parity(3), :], m.xT16[:, s.batch(3), :]).then_inc(tokens_ready, 1)

            pipeline(pool, plan, step)

        @block.tensor
        def _(pe):
            def step(s):
                if s.has(0):
                    a = s.parity(0)
                    pe.wait_ge(kv_ready, s.n(0, 1, 1))
                    if s.known(0, 1):
                        pe.wait_ge(total_copied, s.n(0))
                    for i in range(2):
                        f = slice(i * FREQS, (i + 1) * FREQS)
                        o = psC[0:FREQS, i * SEQ:(i + 1) * SEQ]
                        pe.matmul(o, kv[:, a, 0, f], m.upto[:, :], start=True, stop=False, skip_group_check=True)
                        mm = pe.matmul(o[:, P:SEQ], kv[:, a, 1, f], m.upto[:, 0:P], start=False, stop=True, skip_group_check=True)
                    mm.then_inc(total_ready, 1)
                if s.has(2):
                    c = s.parity(2)
                    pe.wait_ge(tokens_ready, s.n(2, 1, 1))
                    if s.known(2, 1):
                        pe.wait_ge(kqv_ready, s.n(2))
                    for t in range(2):
                        mm = pe.matmul(psP[t][:, 0:3 * F2], xcur[:, c, t * P:(t + 1) * P], w.kqv[:, :], start=True, stop=True)
                    mm.then_inc(projected, 1)
                if s.has(0):
                    pe.wait_ge(final_ready, s.n(0, 1, 1))
                    if s.known(0, 1):
                        pe.wait_ge(x_updated, s.n(0))
                    for t in range(2):
                        for i in range(2):
                            mm = pe.matmul(psX[:, t * D:(t + 1) * D], final[:, i, t * P:(t + 1) * P], w.back[:, i, :], start=(i == 0), stop=(i == 1))
                    mm.then_inc(out_ready, 1)
                if s.has(1):
                    c = s.parity(1)
                    pe.wait_ge(unit_ready, s.n(1, 1, 1))
                    if s.known(1, 1):
                        pe.wait_ge(qT_ready, s.n(1))
                    for i in range(2):
                        for t in range(2):
                            mm = pe.transpose(psQ[0:FREQS, i * SEQ + t * P:i * SEQ + (t + 1) * P],
                                              kqv[:, c, t, F2 + i * FREQS:F2 + (i + 1) * FREQS], m.identity[:, :])
                    mm.then_inc(q_turned, 1)

            pipeline(pe, plan, step)

        @block.scalar
        def _(act):
            def step(s):
                if s.has(0):
                    act.wait_ge(total_ready, s.n(0, 1, 1))
                    if s.known(0, 1):
                        act.wait_ge(final_ready, s.n(0))
                    act.activation(total[:, :, :], psC[0:FREQS, :], ACT.Copy).then_inc(total_copied, 1)
                if s.has(1):
                    act.wait_ge(power_ready, s.n(1, 1, 1))
                    act.activation(size[:, :, :, :], power[:, :, :, :], ACT.Sqrt).then_inc(size_ready, 1)
                if s.has(2):
                    c = s.parity(2)
                    act.wait_ge(projected, s.n(2, 1, 1))
                    if s.known(2, 1):
                        act.wait_ge(power_ready, s.n(2))
                    if s.known(2, 2):
                        act.wait_ge(q_turned, s.n(2, 1, -1))
                    for t in range(2):
                        act.activation(square[:, t, :], psP[t][:, 0:2 * F2], ACT.Square)
                        k = act.activation(kqv[:, c, t, :], psP[t][:, 0:3 * F2], ACT.Copy)
                    k.then_inc(kqv_ready, 1)
                if s.has(1):
                    act.wait_ge(q_turned, s.n(1, 1, 1))
                    if s.known(1, 1):
                        act.wait_ge(final_ready, s.n(1))
                    act.activation(qT[:, :, :], psQ[0:FREQS, :], ACT.Copy).then_inc(qT_ready, 1)

            pipeline(act, plan, step)

        @block.vector
        def _(dve):
            def step(s):
                if s.has(1):
                    c = s.parity(1)
                    dve.wait_ge(kqv_ready, s.n(1, 1, 1))
                    sq = square[:, :, :].rearrange("p t (c i f) -> p t c i f", c=2, i=2)
                    dve.tensor_tensor(power[:, :, :, :], sq[:, :, :, 0, :], sq[:, :, :, 1, :], ALU.add).then_inc(power_ready, 1)
                if s.has(0):
                    dve.wait_ge(total_copied, s.n(0, 1, 1))
                    dve.wait_ge(qT_ready, s.n(0, 1, 1))
                    dve.tensor_tensor(straight[:, :, :], total[:, :, :], qT[:, :, :], ALU.mult).then_inc(across_ready, 1)
                    dve.tensor_tensor(across[:, 0, :], total[:, 1, :], qT[:, 0, :], ALU.mult).then_inc(across_ready, 1)
                    dve.tensor_tensor(across[:, 1, :], total[:, 0, :], qT[:, 1, :], ALU.mult).then_inc(across_ready, 1)
                    dve.wait_ge(across_ready, s.n(0, 3, 3))
                    if s.known(0, 1):
                        dve.wait_ge(out_ready, s.n(0))
                    dve.tensor_tensor(final[:, 0, :], straight[:, 0, :], straight[:, 1, :], ALU.add)
                    dve.tensor_tensor(final[:, 1, :], across[:, 0, :], across[:, 1, :], ALU.subtract).then_inc(final_ready, 1)
                if s.has(1):
                    c = s.parity(1)
                    dve.wait_ge(size_ready, s.n(1, 1, 1))
                    dve.tensor_scalar(size[:, :, :, :], size[:, :, :, :], 1e-8, None, ALU.add).then_inc(dve_step, 1)
                    dve.wait_ge(dve_step, s.n(1, 7, 1))
                    dve.reciprocal(inverse[:, :, :, :], size[:, :, :, :]).then_inc(dve_step, 1)
                    dve.wait_ge(dve_step, s.n(1, 7, 2))
                    for i, part in enumerate((K, Q)):
                        a = halves(kqv[:, c, :, part])
                        u = dve.tensor_tensor(a, a, inverse[:, :, i, :].unsqueeze(2).to_broadcast([P, 2, 2, FREQS]), ALU.mult)
                        u.then_inc(unit_ready if i else dve_step, 1)
                    dve.wait_ge(dve_step, s.n(1, 7, 3))
                    k, v = kqv[:, c, :, K], kqv[:, c, :, V]
                    k2, v2 = halves(k), halves(v)
                    dve.tensor_tensor(prod[:, :, :], k, v, ALU.mult).then_inc(dve_step, 1)
                    dve.tensor_tensor(cross[:, :, 0, :], k2[:, :, 0, :], v2[:, :, 1, :], ALU.mult).then_inc(dve_step, 1)
                    dve.tensor_tensor(cross[:, :, 1, :], k2[:, :, 1, :], v2[:, :, 0, :], ALU.mult).then_inc(dve_step, 1)
                    dve.wait_ge(dve_step, s.n(1, 7, 6))
                    if s.known(1, 2):
                        dve.wait_ge(total_ready, s.n(1, 1, -1))
                    p2 = halves(prod[:, :, :])
                    dve.tensor_tensor(kv[:, c, :, 0:FREQS], p2[:, :, 0, :], p2[:, :, 1, :], ALU.subtract).then_inc(dve_step, 1)
                    dve.tensor_tensor(kv[:, c, :, FREQS:F2], cross[:, :, 0, :], cross[:, :, 1, :], ALU.add).then_inc(kv_ready, 1)
                if s.has(0):
                    dve.wait_ge(out_ready, s.n(0, 1, 1))
                    b = s.batch(0)
                    dve.tensor_tensor(m.x16[:, b, :], psX[:, 0:SEQ], m.x16[:, b, :], ALU.add).then_inc(x_updated, 1)
                    dve.wait_ge(x_updated, s.n(0, 1, 1))
                    batch_stats(dve, m, b).then_inc(stats_done, 1)

            pipeline(dve, plan, step)


def router(nc, m, w):
    with ExitStack() as ctx:
        sem, sb, begin = stage(nc, ctx, "router")
        logitsT = sb("logitsT", [EXPERTS, TILES * P])
        lg = sb("lg", [P, TILES, EXPERTS])
        prob = sb("prob", [P, TILES, EXPERTS])
        rank = sb("rank", [P, TILES, EXPERTS])
        member = sb("member", [P, TILES, EXPERTS])
        compare = sb("compare", [P, 12, TILES])
        col = sb("col", [P, 3, TILES])
        anyone = sb("anyone", [P, BATCHES, 2, EXPERTS])
        counts = sb("counts", [P, BATCHES, 2, EXPERTS])
        mask = sb("mask", [P, 2, BATCHES, EXPERTS])
        maskT = sb("maskT", [P, P], BF16)
        psL = [ctx.enter_context(nc.psum_tensor(f"router_psL{k}", [P, 512], F32)) for k in range(2)]
        psT = ctx.enter_context(nc.psum_tensor("router_psT", [P, 512], F32))
        logits_ready, logitsT_ready, turned, step_done, top_ready, exp_ready, member_ready, counted, mask_ready, mask_turned, maskT_ready, saved = (
            sem(n) for n in ("logits_ready", "logitsT_ready", "turned", "step_done", "top_ready", "exp_ready", "member_ready",
                             "counted", "mask_ready", "mask_turned", "maskT_ready", "saved"))
        block = begin()

        @block.tensor
        def _(pe):
            for g in range(GROUPS):
                if g >= 2:
                    pe.wait_ge(logitsT_ready, g - 1)
                pe.matmul(psL[g % 2][0:EXPERTS, :], w.router[:, :], m.xT8[:, g, :], start=True, stop=True).then_inc(logits_ready, 1)
            pe.wait_ge(logitsT_ready, GROUPS)
            for t in range(TILES):
                mm = pe.transpose(psT[:, EXPERTS * t:EXPERTS * (t + 1)], logitsT[:, t * P:(t + 1) * P], m.identity[0:EXPERTS, 0:EXPERTS])
            mm.then_inc(turned, 1)
            pe.wait_ge(member_ready, 1)
            pe.matmul(psL[0][:, 0:P], m.ones[:, :], member[:, :, :].rearrange("p t e -> p (t e)"), start=True, stop=True).then_inc(counted, 1)
            pe.wait_ge(mask_ready, 1)
            pe.transpose(psL[1][:, 0:P], mask[:, :, :, :].rearrange("p t b e -> p (t b e)"), m.identity[:, :]).then_inc(mask_turned, 1)

        @block.scalar
        def _(act):
            for g in range(GROUPS):
                act.wait_ge(logits_ready, g + 1)
                act.activation(logitsT[:, g * 512:(g + 1) * 512], psL[g % 2][0:EXPERTS, :], ACT.Identity, bias=w.router_b[:, 0:1]).then_inc(logitsT_ready, 1)
            act.wait_ge(top_ready, 1)
            act.activation(prob[:, :, :], lg[:, :, :], ACT.Exp).then_inc(exp_ready, 1)
            act.wait_ge(mask_turned, 1)
            act.activation(maskT[:, :], psL[1][:, 0:P], ACT.Copy).then_inc(maskT_ready, 1)

        @block.sync
        def _(sp):
            sp.wait_ge(maskT_ready, 1)
            for t in range(2):
                rows = slice(t * BATCHES * EXPERTS, (t + 1) * BATCHES * EXPERTS)
                sp.dma_start(m.mask_dram.rearrange("b e k -> (b e) k")[:, t * P:(t + 1) * P], maskT[rows, :]).then_inc(saved, 16)
            sp.wait_ge(saved, 32)

        @block.vector
        def _(dve):
            n = [0]

            def chain(ins):
                n[0] += 1
                ins.then_inc(step_done, 1)
                dve.wait_ge(step_done, n[0])

            dve.wait_ge(turned, 1)
            logits = psT[:, 0:TILES * EXPERTS].rearrange("p (t e) -> p t e", e=EXPERTS)
            over_e = lambda a: a.unsqueeze(2).to_broadcast([P, TILES, EXPERTS])
            chain(dve.tensor_reduce(col[:, 0, :], logits, AX_X, ALU.max))
            dve.tensor_tensor(lg[:, :, :], logits, over_e(col[:, 0, :]), ALU.subtract).then_inc(top_ready, 1)
            dve.wait_ge(exp_ready, 1)
            chain(dve.tensor_reduce(col[:, 1, :], prob[:, :, :], AX_X, ALU.add))
            chain(dve.reciprocal(col[:, 2, :], col[:, 1, :]))
            chain(dve.tensor_tensor(prob[:, :, :], prob[:, :, :], over_e(col[:, 2, :]), ALU.mult))
            k = 0
            for e in range(EXPERTS):
                for o in range(EXPERTS):
                    if o != e:
                        last = dve.tensor_tensor(compare[:, k, :], prob[:, :, o], prob[:, :, e], ALU.is_ge if o < e else ALU.is_gt)
                        k += 1
            chain(last)
            for e in range(EXPERTS):
                last = dve.tensor_tensor(rank[:, :, e], compare[:, 3 * e, :], compare[:, 3 * e + 1, :], ALU.add)
            chain(last)
            for e in range(EXPERTS):
                last = dve.tensor_tensor(rank[:, :, e], rank[:, :, e], compare[:, 3 * e + 2, :], ALU.add)
            chain(last)
            dve.tensor_scalar(member[:, :, :], rank[:, :, :], 2.0, None, ALU.is_lt).then_inc(member_ready, 1)
            dve.wait_ge(member_ready, 1)
            dve.tensor_tensor(m.gate[:, :, :, :].rearrange("p b t e -> p (b t) e"), prob[:, :, :], member[:, :, :], ALU.mult)
            dve.wait_ge(counted, 1)
            chain(dve.tensor_copy(counts[:, :, :, :].rearrange("p b t e -> p (b t e)"), psL[0][:, 0:P]))
            for t in range(2):
                last = dve.tensor_tensor(anyone[:, :, t, :], counts[:, :, 0, :], counts[:, :, 1, :], ALU.add)
            chain(last)
            chain(dve.tensor_scalar(anyone[:, :, :, :].rearrange("p b t e -> p (b t e)"), anyone[:, :, :, :].rearrange("p b t e -> p (b t e)"), 1.0, NEG, ALU.min, ALU.mult))
            chain(dve.tensor_scalar(member[:, :, :], member[:, :, :], -1.0, 1.0, ALU.mult, ALU.add))
            dve.tensor_tensor(mask[:, :, :, :].rearrange("p t b e -> p b t e"), member[:, :, :].rearrange("p (b t) e -> p b t e", t=2),
                              anyone[:, :, :, :], ALU.mult).then_inc(mask_ready, 1)


def fill_stacks(m, sem, block):
    ones_ready, stacks_zero, rows_set = sem("ones_ready"), sem("stacks_zero"), sem("rows_set")

    @block.gpsimd
    def _(pool):
        pool.memset(m.ones_bf[:, :], 1.0).then_inc(ones_ready, 1)
        pool.memset(m.stackq[:, :, :, :], 0.0).then_inc(stacks_zero, 1)
        pool.memset(m.stackk[:, :, :, :], 0.0).then_inc(stacks_zero, 1)

    @block.sync
    def _(sp):
        sp.wait_ge(ones_ready, 1)
        sp.wait_ge(stacks_zero, 2)
        rows = [m.stackq[MASK_ROW:MASK_ROW + 1, :, :, :]] + [m.stackk[r:r + 1, :, :, :] for r in (MAX_ROW, MAX_ROW + 1)]
        for row in rows:
            sp.dma_start(row, m.ones_bf[:, 0:2 * HEADS * SEQ // P]).then_inc(rows_set, 16)
        sp.wait_ge(rows_set, 16 * len(rows))


def load(nc, m, a):
    W = Weights
    ctx = m.ctx
    sb = lambda n, s, dt=F32: ctx.enter_context(nc.sbuf_tensor(n, s, dt))
    x = sb("x", [P, TILES, D])
    m.x4 = x[:, :, :].rearrange("p (g k) d -> p g k d", k=4)
    m.xg = x[:, :, :].rearrange("p (g k) d -> p g (k d)", k=4)
    m.x16 = x[:, :, :].rearrange("p (b t) d -> p b (t d)", t=2)
    m.x32 = x[:, :, :].rearrange("p (b t) d -> p b t d", t=2)
    xT = sb("xT", [P, TILES * P])
    m.xT8 = xT[:, :].rearrange("p (g n) -> p g n", n=512)
    m.xT16 = xT[:, :].rearrange("p (b n) -> p b n", n=SEQ)
    m.identity, m.identity_bf, m.ones = sb("identity", [P, P]), sb("identity_bf", [P, P], BF16), sb("ones", [P, P])
    m.causal, m.upto = sb("causal", [P, P], BF16), sb("upto", [P, SEQ])
    m.stats = sb("stats", [P, TILES, 6])
    m.stats4 = m.stats[:, :, :].rearrange("p (g k) c -> p g k c", k=4)
    m.stats2 = m.stats[:, :, :].rearrange("p (b t) c -> p b t c", t=2)
    m.gate = sb("gate", [P, BATCHES, 2, EXPERTS])
    m.mask_dram = nc.dram_tensor("mask_dram", (BATCHES, EXPERTS, SEQ), BF16, kind="Internal").ap()

    m.stackq, m.stackk = sb("stackq", [P, 2, HEADS, SEQ], BF16), sb("stackk", [P, 2, HEADS, SEQ], BF16)
    m.ones_bf = sb("ones_bf", [P, P], BF16)
    m.values = sb("values", [P, 2, 2, HEADS, SLOT])

    loads = []

    def held(name, shape, src, dt=F32):
        t = sb(name, shape, dt)
        full = t[tuple(slice(None) for _ in shape)]
        loads.append((full, src))
        return t

    def row_matrix(name, shape, src):
        t = sb(name, shape)
        rows.append(t)
        row_loads.append((t[0:1, :, :] if len(shape) == 3 else t[0:1, :], src))
        return t

    rows, row_loads = [], []
    bcast = lambda ap, n: ap.unsqueeze(0).to_broadcast([P, n])
    l0 = W(wq=held("l0_wq", [P, 1024], a["l0_w"][:, 0]), wk=held("l0_wk", [P, 1024], a["l0_w"][:, 1]), wv=held("l0_wv", [P, 1024], a["l0_w"][:, 2]),
           bqk=held("l0_bqk", [P, L0_PAIRS, 3], a["l0_bqk"]), bv=held("l0_bv", [P, 1024], bcast(a["l0_bv"], 1024)),
           wo=held("l0_wo", [P, L0_PAIRS, D], a["l0_wo"]), bo=row_matrix("l0_bo", [P, D], a["l0_bo"].unsqueeze(0)))
    l0_loads = len(loads)
    ffn, ints = [], []
    for i in range(2):
        f = W(gate=sb(f"f{i}_gate", [P, HIDDEN]), up=sb(f"f{i}_up", [P, HIDDEN]), down=sb(f"f{i}_down", [P, HCH, D]))
        for n, t, shape in (("gate", f.gate, [P, HIDDEN]), ("up", f.up, [P, HIDDEN]), ("down", f.down, [P, HCH, D])):
            loads.append((t[:, :].bitcast(I32) if len(shape) == 2 else t[:, :, :].bitcast(I32), a[f"f{i}_{n}"]))
            ints.append(t[:, :] if len(shape) == 2 else t[:, :, :])
        ffn.append(f)

    def heads8(name, weights):
        return dict(wq=held(f"{name}_wq", [P, weights, D], a[f"{name}_wq"]), wk=held(f"{name}_wk", [P, weights, D], a[f"{name}_wk"]),
                    wv=held(f"{name}_wv", [P, weights, D], a[f"{name}_wv"]), wo=held(f"{name}_wo", [P, weights, D], a[f"{name}_wo"]),
                    bv=held(f"{name}_bv", [P, weights, D], a[f"{name}_bv"].unsqueeze(0).to_broadcast([P, weights, D])),
                    bo=row_matrix(f"{name}_bo", [P, weights, D], a[f"{name}_bo"].unsqueeze(0)),
                    bo_parts=sb(f"{name}_bo_parts", [P, 3, weights, D], BF16))

    l1 = W(**heads8("l1", 1), bq=held("l1_bq", [P, 1], a["l1_bq"]), bk=held("l1_bk", [P, 1], a["l1_bk"]), exp_scale=1.0, ones_value=float(np.sqrt(np.float32(D))))
    l2 = W(**heads8("l2", EXPERTS), bq=held("l2_bq", [P, EXPERTS], a["l2_bq"]), bk=held("l2_bk", [P, EXPERTS], a["l2_bk"]), exp_scale=0.5, ones_value=1.0,
           router=held("l2_router", [P, EXPERTS], a["router_w"]), router_b=held("l2_router_b", [EXPERTS, 1], a["router_b"].unsqueeze(1)))
    l3 = W(**heads8("l3", 1), wq2=held("l3_wq2", [P, 1, D], a["l3_wq2"]), wk2=held("l3_wk2", [P, 1, D], a["l3_wk2"]),
           rot_bias=held("l3_rb", [P, 4], a["l3_rb"]), tables=held("l3_tables", [P, 2, 2, SEQ], a["c_rotary"]), exp_scale=1.0, ones_value=1.0)
    fold_in = held("fold_in", [P, 3, D], a["l2a_w"])
    dft = held("dft", [P, 2 * FREQS], a["c_dft"])
    fa = W(kqv=sb("fa_kqv", [P, 3 * 2 * FREQS]), back=held("fa_back", [FREQS, 2, D], a["c_idft"]))
    ku = [held("k0_bytes", [P, 2, FF3 // 4], a["k0"], I32)[:, :, :].bitcast(U8), held("k1_bytes", [P, 4, FF3 // 4], a["k1"], I32)[:, :, :].bitcast(U8),
          held("k2_bytes", [P, 4, D // 4], a["k2"], I32)[:, :, :].bitcast(U8)]
    mlp = W(k0=sb("k0", [P, FF3]), k1=sb("k1", [P, 4, FF3]), k2=sb("k2", [P, 4, D]), s=sb("s", [P, 3]))
    s_in = held("s_in", [P, 3], bcast(a["s"], 3))

    m.l0_loaded, m.rest_loaded = ctx.enter_context(nc.semaphore("l0_loaded")), ctx.enter_context(nc.semaphore("rest_loaded"))
    m.l0_loads = 16 * (l0_loads + 1)
    m.later_loads = loads[l0_loads:] + row_loads[1:]
    m.rest_loads = 16 * (len(loads) - l0_loads + len(rows) - 1)

    with ExitStack() as inner:
        sem, _, begin = stage(nc, inner, "load")
        x_loaded, zeroed, pool_step = sem("x_loaded"), sem("zeroed"), sem("pool_step")
        block = begin()

        @block.sync
        def _(sp):
            sp.dma_start(x[:, :, :], a["x"].rearrange("(t p) d -> p t d", p=P)).then_inc(x_loaded, 16)
            for dst, src in loads[:l0_loads]:
                sp.dma_start(dst, src).then_inc(m.l0_loaded, 16)
            sp.wait_ge(zeroed, 1)
            sp.dma_start(*row_loads[0]).then_inc(m.l0_loaded, 16)
            sp.wait_ge(x_loaded, 16)

        @block.vector
        def _(dve):
            for t in rows:
                last = dve.memset(t[:, :, :] if len(t.shape) == 3 else t[:, :], 0.0)
            last.then_inc(zeroed, 1)
            dve.memset(m.values[:, :, :, :, :], 0.0)

        @block.gpsimd
        def _(pool):
            pool.memset(m.identity[:, :], 0.0)
            pool.memset(m.ones[:, :], 1.0)
            pool.memset(m.causal[:, :], 0.0)
            pool.memset(m.upto[:, :], 1.0).then_inc(pool_step, 1)
            pool.wait_ge(pool_step, 1)
            pool.affine_select(out=m.identity[:, :], in_=m.identity[:, :], compare_op=ALU.not_equal, fill=1.0, base=0,
                               pattern=[[-1, P]], channel_multiplier=1).then_inc(pool_step, 1)
            pool.affine_select(out=m.causal[:, :], in_=m.causal[:, :], compare_op=ALU.is_ge, fill=NEG, base=0,
                               pattern=[[1, P]], channel_multiplier=-1)
            pool.affine_select(out=m.upto[:, 0:P], in_=m.upto[:, 0:P], compare_op=ALU.is_ge, fill=0.0, base=0,
                               pattern=[[1, P]], channel_multiplier=-1).then_inc(pool_step, 1)
            pool.wait_ge(pool_step, 2)
            pool.tensor_copy(m.identity_bf[:, :], m.identity[:, :]).then_inc(pool_step, 1)

    def prepare():
        with ExitStack() as inner:
            sem, _, begin = stage(nc, inner, "prepare")
            made, folded, split_step = sem("made"), sem("folded"), sem("split_step")
            psF = inner.enter_context(nc.psum_tensor("prepare_psF", [P, 512], F32))
            block = begin()

            @block.tensor
            def _(pe):
                pe.wait_ge(m.rest_loaded, m.rest_loads)
                for i in range(3):
                    mm = pe.matmul(psF[:, i * 2 * FREQS:(i + 1) * 2 * FREQS], fold_in[:, i, :], dft[:, :], start=True, stop=True)
                mm.then_inc(folded, 1)

            @block.vector
            def _(dve):
                dve.wait_ge(m.rest_loaded, m.rest_loads)
                for t in ints:
                    dve.tensor_scalar(t, t.bitcast(I32), float(np.float32(1.0 / 127.0)), None, ALU.mult)
                for k in range(3):
                    for w in (l1, l2, l3):
                        part = dve.tensor_copy(w.bo_parts[:, k, :, :], w.bo[:, :, :])
                    if k < 2:
                        part.then_inc(split_step, 1)
                        dve.wait_ge(split_step, 2 * k + 1)
                        for w in (l1, l2, l3):
                            rest = dve.tensor_tensor(w.bo[:, :, :], w.bo[:, :, :], w.bo_parts[:, k, :, :], ALU.subtract)
                        rest.then_inc(split_step, 1)
                        dve.wait_ge(split_step, 2 * k + 2)
                dve.tensor_scalar(mlp.s[:, 0:2], s_in[:, 0:2], 2.0, None, ALU.mult)
                dve.tensor_copy(mlp.s[:, 2:3], s_in[:, 2:3])
                dve.tensor_tensor(mlp.k0[:, :], ku[0][:, 0, :], ku[0][:, 1, :], ALU.subtract).then_inc(made, 1)
                dve.tensor_scalar(mlp.k1[:, :, :], ku[1][:, :, :], 2.0, -1.0, ALU.mult, ALU.add)
                dve.tensor_scalar(mlp.k2[:, :, :], ku[2][:, :, :], 2.0, -1.0, ALU.mult, ALU.add)
                dve.wait_ge(made, 1)
                dve.tensor_scalar(mlp.k0[:, :], mlp.k0[:, :], 2.0, None, ALU.mult)
                dve.wait_ge(folded, 1)
                dve.tensor_copy(fa.kqv[:, :], psF[:, 0:6 * FREQS])

    m.prepare = prepare
    m.l0, m.ffn, m.l1, m.l2, m.l3, m.fa, m.mlp = l0, ffn, l1, l2, l3, fa, mlp


def network(nc, a, out):
    m = Model(ExitStack())
    with m.ctx:
        load(nc, m, a)
        layer_norm(nc, m, "n0", rms=True, first=True, meanwhile=fill_stacks)
        attention64(nc, m, m.l0)
        m.prepare()
        layer_norm(nc, m, "n1")
        swiglu(nc, m, "f0", m.ffn[0])
        layer_norm(nc, m, "n2")
        attention8(nc, m, "a1", m.l1)
        layer_norm(nc, m, "n3")
        swiglu(nc, m, "f1", m.ffn[1])
        layer_norm(nc, m, "n4", add_to_x=True)
        fourier_attention(nc, m, m.fa)
        layer_norm(nc, m, "n5")
        router(nc, m, m.l2)
        attention8(nc, m, "a2", m.l2, weights=EXPERTS, masked=True)
        layer_norm(nc, m, "n6")
        attention8(nc, m, "a3", m.l3, rotary=True, clear_mask=True)
        layer_norm(nc, m, "n7")
        sign_mlp(nc, m, m.mlp)
        with nc.semaphore("stored") as stored, nc.Block() as block:
            @block.sync
            def _(sp):
                sp.dma_start(out.rearrange("(b t p) d -> p b t d", t=2, p=P), m.x32).then_inc(stored, 16)
                sp.wait_ge(stored, 16)


def constants():
    n, f = np.arange(D), np.arange(FREQS)
    angle = 2 * np.pi * ((n[:, None] * f[None, :]) % D) / D
    dft = np.concatenate([np.cos(angle), -np.sin(angle)], axis=1)
    dft[:, FREQS] = 0.0
    dft[:, 2 * FREQS - 1] = 0.0
    weight = np.where((f == 0) | (f == FREQS - 1), 1.0, 2.0)[:, None] / D
    idft = np.stack([weight * np.cos(angle.T), -weight * np.sin(angle.T)], axis=1)
    idft[0, 1, :] = 0.0
    idft[FREQS - 1, 1, :] = 0.0
    freqs = 10000.0 ** (np.arange(0, HD, 2) / HD)
    turn = (np.arange(SEQ)[None, :] * np.round(freqs)[:, None])
    cos, sin = np.cos(turn), np.sin(turn)
    rot = np.stack([np.concatenate([cos, cos]), np.concatenate([-sin, sin])])
    scale = np.array([np.float32(HD ** -0.5), 1.0])
    tables = np.repeat(rot[:, :, None, None, :] * scale[None, None, None, :, None], HEADS, axis=2)
    tables = tables.transpose(1, 2, 0, 3, 4).reshape(P, 2, 2, SEQ)
    return dft.astype(np.float32), idft.astype(np.float32), tables.astype(np.float32)


def lay_out(i):
    a = {k: np.asarray(v) for k, v in i.items()}
    c = np.ascontiguousarray
    o = {"x": a["L0_attn_x"].reshape(-1, D)}
    o["l0_w"] = a["L0_attn_W_qkv"].reshape(L0_HEADS, L0_HD, 3, D).transpose(3, 2, 0, 1).reshape(D, 3, 1024)
    b = a["L0_attn_b_qkv"].reshape(L0_PAIRS, 2, L0_HD, 3)
    o["l0_bqk"] = b.transpose(1, 2, 0, 3).reshape(P, L0_PAIRS, 3)
    o["l0_bv"] = b[:, :, :, 2].reshape(1024)
    o["l0_wo"] = a["L0_attn_W_o"].T.reshape(L0_PAIRS, P, D).transpose(1, 0, 2)
    o["l0_bo"] = a["L0_attn_b_o"]
    for n in range(2):
        o[f"f{n}_gate"] = a[f"L{n}_ffn_w_gate"].T
        o[f"f{n}_up"] = a[f"L{n}_ffn_w_up"].T
        o[f"f{n}_down"] = a[f"L{n}_ffn_w_down"].T.reshape(HCH, P, D).transpose(1, 0, 2)
    dh = lambda w: w.reshape(w.shape[:-1] + (HEADS, HD)).swapaxes(-1, -2).reshape(w.shape)

    w, b = a["L1_attn_W_qkv"], a["L1_attn_b_qkv"]
    o["l1_wq"], o["l1_wk"], o["l1_wv"], o["l1_wo"] = dh(w[:, 0:D])[:, None], dh(w[:, D:2 * D])[:, None], w[:, None, 2 * D:], a["L1_attn_W_out"][:, None]
    o["l1_bq"], o["l1_bk"], o["l1_bv"], o["l1_bo"] = dh(b[0:D])[:, None], dh(b[D:2 * D])[:, None], b[None, 2 * D:], a["L1_attn_b_out"][None]
    for n in "qkvo":
        w = a[f"L2_ffn_w{n}"].transpose(1, 0, 2)
        o[f"l2_w{n}"] = dh(w) if n in "qk" else w
    o["l2_bq"], o["l2_bk"] = dh(a["L2_ffn_bq"]).T, dh(a["L2_ffn_bk"]).T
    o["l2_bv"], o["l2_bo"] = a["L2_ffn_bv"], a["L2_ffn_bo"]
    o["router_w"], o["router_b"] = a["L2_ffn_router_w"], a["L2_ffn_router_b"]
    o["l2a_w"] = np.stack([a["L2_attn_Wk"], a["L2_attn_Wq"], a["L2_attn_Wv"]], axis=1)

    def rotated(w, partner):
        v = w.reshape(w.shape[:-1] + (HEADS, HD // 2, 2))
        v = np.moveaxis(v, (-1, -2, -3), (-3, -2, -1))
        if partner:
            v = v[..., ::-1, :, :]
        return v.reshape(w.shape)

    w, b = a["L3_attn_qkv_w"], a["L3_attn_qkv_b"]
    for n, at in (("q", 0), ("k", D)):
        o[f"l3_w{n}"], o[f"l3_w{n}2"] = rotated(w[:, at:at + D], False)[:, None], rotated(w[:, at:at + D], True)[:, None]
    o["l3_rb"] = np.stack([rotated(b[0:D], False), rotated(b[D:2 * D], False), rotated(b[0:D], True), rotated(b[D:2 * D], True)], axis=1)
    o["l3_wv"], o["l3_wo"], o["l3_bv"], o["l3_bo"] = w[:, None, 2 * D:], a["L3_attn_out_w"][:, None], b[None, 2 * D:], a["L3_attn_out_b"][None]
    for n, k in (("k0", 2), ("k1", 4), ("k2", 4)):
        fours = c(a[f"L3_ffn_{n}"]).view(np.int32)
        o[n] = fours.reshape(k, P, fours.shape[1]).transpose(1, 0, 2)
    o["s"] = np.stack([a["L3_ffn_s0"], a["L3_ffn_s1"], a["L3_ffn_s2"]])
    o["c_dft"], o["c_idft"], o["c_rotary"] = constants()
    return {k: c(v) for k, v in o.items()}


def kernel(**inputs):
    import concourse.bacc as bacc
    from concourse.bass_utils import run_bass_kernel_spmd

    arrays = lay_out(inputs)
    nc = bacc.Bacc("TRN2", target_bir_lowering=False, num_devices=1)
    a = {k: nc.dram_tensor(f"in_{k}", v.shape, mybir.dt.from_np(v.dtype), kind="ExternalInput").ap() for k, v in arrays.items()}
    out = nc.dram_tensor("out", (BATCHES * SEQ, D), F32, kind="ExternalOutput").ap()
    network(nc, a, out)
    r = run_bass_kernel_spmd(nc, [{f"in_{k}": v for k, v in arrays.items()}], core_ids=[0])
    return np.asarray(r.results[0]["out"]).reshape(BATCHES, SEQ, D)
```
